# Optimizing a Trainium2 kernel written in Bass

```python
import numpy as np
import jax
import jax.numpy as jnp

def _softmax(x, axis=-1):
    return jax.nn.softmax(x, axis=axis)

def _gelu(x):
    return jax.nn.gelu(x, approximate=True)

def _silu(x):
    return jax.nn.silu(x)

def _sigmoid(x):
    return jax.nn.sigmoid(x)

def _layernorm(x, axis=-1, eps=1e-05):
    m = jnp.mean(x, axis=axis, keepdims=True)
    v = jnp.var(x, axis=axis, keepdims=True)
    return (x - m) / jnp.sqrt(v + eps)

def _scatter_add(tgt, idx, src, axis=0):
    return tgt.at[idx].add(src)

def _segment_sum(src, seg, n):
    return jax.ops.segment_sum(src, seg, n)
kernel_name = 'mk_audio_tower_d2_tok_audfeat256_r4_2457f8'

def setup_inputs(seed: int=0):
    np.random.seed(seed)
    _w = jnp.asarray

    def _rec_inputs():
        import jax
        import jax.numpy as jnp
        _rk = jax.random.key(seed)
        x = -0.000392918 + 0.999932 * jax.random.normal(jax.random.fold_in(_rk, 1), (8, 375, 128), jnp.float32)
        return x
    x = _rec_inputs()

    def _L0_tok_setup():
        import jax, jax.numpy as jnp
        import numpy as np
        EPS = 1e-07
        K = 15
        CIN = 128
        F = 64
        key = jax.random.key(seed)
        k1, k2 = jax.random.split(key)
        x = jax.random.normal(k1, (32, 1024, CIN), dtype=jnp.float32)
        limit = np.sqrt(6.0 / (K * CIN + F))
        kernel = jax.random.uniform(k2, (K, CIN, F), dtype=jnp.float32, minval=-limit, maxval=limit)
        kernel = kernel / jnp.sqrt(jnp.sum(kernel * kernel, axis=(0, 1), keepdims=True) + 1e-12)
        scale = jnp.full((1, 1, 1), 10.0, dtype=jnp.float32)
        bias = jnp.zeros((F,), dtype=jnp.float32)
        return {'inputs': x, 'kernel': kernel, 'scale': scale, 'bias': bias}
    _L0_tok_all = _L0_tok_setup()
    _L0_tok_in = {k: v for k, v in _L0_tok_all.items() if k in ('kernel', 'scale', 'bias')}
    del _L0_tok_all

    def _L0_attn_setup():
        import jax, jax.numpy as jnp
        import numpy as np
        import math
        B, N, D = (4, 1024, 64)
        key = jax.random.key(seed)
        k0, k1, k2, k3 = jax.random.split(key, 4)
        bound = math.sqrt(6.0 / D)
        return {'x': jax.random.normal(k0, (B, N, D), dtype=jnp.float32), 'Wq': jax.random.uniform(k1, (D, D), dtype=jnp.float32, minval=-bound, maxval=bound), 'Wk': jax.random.uniform(k2, (D, D), dtype=jnp.float32, minval=-bound, maxval=bound), 'Wv': jax.random.uniform(k3, (D, D), dtype=jnp.float32, minval=-bound, maxval=bound)}
    _L0_attn_all = _L0_attn_setup()
    _L0_attn_in = {k: v for k, v in _L0_attn_all.items() if k in ('Wq', 'Wk', 'Wv')}
    del _L0_attn_all

    def _L0_ffn_setup():
        import jax, jax.numpy as jnp
        import numpy as np
        B, S, D = (8, 1024, 64)
        H = 4 * D
        CAPACITY = 0.5
        key = jax.random.key(seed)
        ks = jax.random.split(key, 6)
        x = jax.random.normal(ks[0], (B, S, D), dtype=jnp.float32)
        attention_mask = jnp.zeros((B, 1, 1, S), dtype=jnp.float32)
        wr = jax.random.normal(ks[1], (D, 1), dtype=jnp.float32) * 0.02
        br = jnp.zeros((1,), dtype=jnp.float32)
        w1 = jax.random.normal(ks[2], (D, H), dtype=jnp.float32) * 0.02
        b1 = jnp.zeros((H,), dtype=jnp.float32)
        w2 = jax.random.normal(ks[3], (H, D), dtype=jnp.float32) * 0.02
        b2 = jnp.zeros((D,), dtype=jnp.float32)
        return {'x': x, 'attention_mask': attention_mask, 'wr': wr, 'br': br, 'w1': w1, 'b1': b1, 'w2': w2, 'b2': b2}
    _L0_ffn_all = _L0_ffn_setup()
    _L0_ffn_in = {k: v for k, v in _L0_ffn_all.items() if k in ('attention_mask', 'wr', 'br', 'w1', 'b1', 'w2', 'b2')}
    del _L0_ffn_all

    def _L1_attn_setup():
        import jax, jax.numpy as jnp
        import numpy as np
        U_DECAY = 0.97
        X_DECAY = 0.97
        LN_EPS = 1e-05
        L1_EPS = 1e-12

        def _ln(x):
            m = jnp.mean(x, axis=-1, keepdims=True)
            v = jnp.mean((x - m) ** 2, axis=-1, keepdims=True)
            return (x - m) * jax.lax.rsqrt(v + LN_EPS)
        key = jax.random.key(seed)
        k0, k1, k2, k3 = jax.random.split(key, 4)
        B, T, d, n = (8, 64, 64, 256)
        embeddings = jax.random.normal(k0, (B, T, d), dtype=jnp.float32)
        E = jax.random.normal(k1, (d, n), dtype=jnp.float32) / n ** 0.5
        Dx = jax.random.normal(k2, (n, d), dtype=jnp.float32) / d ** 0.5
        Dy = jax.random.normal(k3, (n, d), dtype=jnp.float32) / d ** 0.5
        return {'embeddings': embeddings, 'E': E, 'Dx': Dx, 'Dy': Dy}
    _L1_attn_all = _L1_attn_setup()
    _L1_attn_in = {k: v for k, v in _L1_attn_all.items() if k in ('E', 'Dx', 'Dy')}
    del _L1_attn_all

    def _L1_ffn_setup():
        import jax, jax.numpy as jnp
        import numpy as np
        TOP_K = 2
        LN_EPS = 1e-05
        key = jax.random.key(seed)
        ks = jax.random.split(key, 8)
        B, S, D, E, H = (16, 256, 64, 8, 256)
        x = jax.random.normal(ks[0], (B, S, D), dtype=jnp.float32)
        Wr = jax.random.normal(ks[1], (D, E), dtype=jnp.float32) * 0.1
        br = jnp.zeros((E,), dtype=jnp.float32)
        ln_g = jnp.ones((E, D), dtype=jnp.float32)
        ln_b = jnp.zeros((E, D), dtype=jnp.float32)
        W1 = jax.random.normal(ks[2], (E, D, H), dtype=jnp.float32) * (1.0 / np.sqrt(D))
        b1 = jnp.zeros((E, H), dtype=jnp.float32)
        W2 = jax.random.normal(ks[3], (E, H, D), dtype=jnp.float32) * (1.0 / np.sqrt(H))
        b2 = jnp.zeros((E, D), dtype=jnp.float32)
        return {'x': x, 'Wr': Wr, 'br': br, 'ln_g': ln_g, 'ln_b': ln_b, 'W1': W1, 'b1': b1, 'W2': W2, 'b2': b2}
    _L1_ffn_all = _L1_ffn_setup()
    _L1_ffn_in = {k: v for k, v in _L1_ffn_all.items() if k in ('Wr', 'br', 'ln_g', 'ln_b', 'W1', 'b1', 'W2', 'b2')}
    del _L1_ffn_all
    return {'x': x, 'L0_tok_kernel': _L0_tok_in['kernel'], 'L0_tok_scale': _L0_tok_in['scale'], 'L0_tok_bias': _L0_tok_in['bias'], 'L0_attn_Wq': _L0_attn_in['Wq'], 'L0_attn_Wk': _L0_attn_in['Wk'], 'L0_attn_Wv': _L0_attn_in['Wv'], 'L0_ffn_attention_mask': _L0_ffn_in['attention_mask'], 'L0_ffn_wr': _L0_ffn_in['wr'], 'L0_ffn_br': _L0_ffn_in['br'], 'L0_ffn_w1': _L0_ffn_in['w1'], 'L0_ffn_b1': _L0_ffn_in['b1'], 'L0_ffn_w2': _L0_ffn_in['w2'], 'L0_ffn_b2': _L0_ffn_in['b2'], 'L1_attn_E': _L1_attn_in['E'], 'L1_attn_Dx': _L1_attn_in['Dx'], 'L1_attn_Dy': _L1_attn_in['Dy'], 'L1_ffn_Wr': _L1_ffn_in['Wr'], 'L1_ffn_br': _L1_ffn_in['br'], 'L1_ffn_ln_g': _L1_ffn_in['ln_g'], 'L1_ffn_ln_b': _L1_ffn_in['ln_b'], 'L1_ffn_W1': _L1_ffn_in['W1'], 'L1_ffn_b1': _L1_ffn_in['b1'], 'L1_ffn_W2': _L1_ffn_in['W2'], 'L1_ffn_b2': _L1_ffn_in['b2']}

def reference(x, L0_tok_kernel, L0_tok_scale, L0_tok_bias, L0_attn_Wq, L0_attn_Wk, L0_attn_Wv, L0_ffn_attention_mask, L0_ffn_wr, L0_ffn_br, L0_ffn_w1, L0_ffn_b1, L0_ffn_w2, L0_ffn_b2, L1_attn_E, L1_attn_Dx, L1_attn_Dy, L1_ffn_Wr, L1_ffn_br, L1_ffn_ln_g, L1_ffn_ln_b, L1_ffn_W1, L1_ffn_b1, L1_ffn_W2, L1_ffn_b2):
    import jax
    import jax.numpy as jnp

    def _L0_tok_ref(inputs, kernel, scale, bias):
        import jax, jax.numpy as jnp
        import numpy as np
        EPS = 1e-07
        K = 15
        CIN = 128
        F = 64
        dot = jax.lax.conv_general_dilated(inputs, kernel, window_strides=(1,), padding='VALID', dimension_numbers=('NWC', 'WIO', 'NWC'))
        k = kernel.shape[0]
        sq = jnp.sum(inputs * inputs, axis=-1)
        cs = jnp.cumsum(jnp.pad(sq, ((0, 0), (1, 0))), axis=1)
        win = cs[:, k:] - cs[:, :-k]
        norm_x = jnp.sqrt(win + EPS)[..., None]
        return scale * (dot / norm_x) + bias

    def _L0_attn_ref(x, Wq, Wk, Wv):
        import jax, jax.numpy as jnp
        import numpy as np
        import math
        B, N, D = (4, 1024, 64)
        q = x @ Wq.T
        k = x @ Wk.T
        v = x @ Wv.T
        n = x.shape[1]
        d_k = x.shape[2]
        mask = jnp.triu(jnp.ones((n, n), dtype=x.dtype), k=1)
        scale = jnp.asarray(1.0 / math.sqrt(d_k), dtype=x.dtype)
        s = (jnp.einsum('bnd,bmd->bnm', q, k) - (1.0 - mask) * 10000000000.0) * scale
        s = jax.nn.softmax(s, axis=1)
        return jnp.einsum('bnm,bmd->bnd', s, v)

    def _L0_ffn_ref(x, attention_mask, wr, br, w1, b1, w2, b2):
        import jax, jax.numpy as jnp
        import numpy as np
        B, S, D = (8, 1024, 64)
        H = 4 * D
        CAPACITY = 0.5
        b, s, d = x.shape
        weights = (jnp.einsum('bsd,do->bso', x, wr) + br)[..., 0]
        k = max(1, int(CAPACITY * s))
        kk = k - 1 if k > 1 else 1
        _, idx = jax.lax.top_k(weights, k)
        sel_idx = idx[:, :kk]
        sel = jnp.take_along_axis(x, sel_idx[:, :, None], axis=1)
        h = jax.nn.gelu(jnp.einsum('bkd,dh->bkh', sel, w1) + b1)
        y = jnp.einsum('bkh,hd->bkd', h, w2) + b2
        w_sel = jnp.take_along_axis(weights, sel_idx, axis=1)
        y = y * w_sel[..., None]
        batch_idx = jnp.arange(b)[:, None]
        processed = jnp.zeros_like(x).at[batch_idx, sel_idx].set(y)
        return processed + x

    def _L1_attn_ref(embeddings, E, Dx, Dy):
        import jax, jax.numpy as jnp
        import numpy as np
        U_DECAY = 0.97
        X_DECAY = 0.97
        LN_EPS = 1e-05
        L1_EPS = 1e-12

        def _ln(x):
            m = jnp.mean(x, axis=-1, keepdims=True)
            v = jnp.mean((x - m) ** 2, axis=-1, keepdims=True)
            return (x - m) * jax.lax.rsqrt(v + LN_EPS)
        B, T, d = embeddings.shape
        n = E.shape[1]

        def step(carry, v_prev):
            x_state, rho = carry
            x_update = jax.nn.relu(v_prev @ Dx.T)
            x_t = X_DECAY * x_state + x_update
            x_t = x_t / jnp.maximum(jnp.sum(jnp.abs(x_t), axis=-1, keepdims=True), L1_EPS)
            a_star = jnp.einsum('bdn,bn->bd', rho, x_t)
            y_core = _ln(a_star) @ Dy.T
            y_t = jax.nn.relu(y_core) * jax.nn.relu(x_t)
            v_star = _ln(y_t @ E.T)
            rho_t = U_DECAY * rho + _ln(v_prev)[:, :, None] * x_t[:, None, :]
            return ((x_t, rho_t), v_star)
        x0 = jnp.zeros((B, n), dtype=embeddings.dtype)
        rho0 = jnp.zeros((B, d, n), dtype=embeddings.dtype)
        _, vs = jax.lax.scan(step, (x0, rho0), jnp.swapaxes(embeddings, 0, 1))
        return jnp.swapaxes(vs, 0, 1)

    def _L1_ffn_ref(x, Wr, br, ln_g, ln_b, W1, b1, W2, b2):
        import jax, jax.numpy as jnp
        import numpy as np
        TOP_K = 2
        LN_EPS = 1e-05
        B, S, D = x.shape
        N = B * S
        xt = x.reshape(N, D)
        logits = xt @ Wr + br
        probs = jax.nn.softmax(logits, axis=-1)
        top_p, top_idx = jax.lax.top_k(probs, TOP_K)
        weights = top_p / top_p.sum(axis=-1, keepdims=True)
        mu = xt.mean(axis=-1, keepdims=True)
        var = ((xt - mu) ** 2).mean(axis=-1, keepdims=True)
        xn = (xt - mu) * jax.lax.rsqrt(var + LN_EPS)
        xe = xn[None, :, :] * ln_g[:, None, :] + ln_b[:, None, :]
        h = jax.nn.gelu(jnp.einsum('end,edh->enh', xe, W1) + b1[:, None, :], approximate=False)
        y = jnp.einsum('enh,ehd->end', h, W2) + b2[:, None, :]
        y_tok = jnp.transpose(y, (1, 0, 2))
        sel = jnp.take_along_axis(y_tok, top_idx[:, :, None], axis=1)
        out = (weights[:, :, None] * sel).sum(axis=1)
        return out.reshape(B, S, D)
    h = _L0_tok_ref(x, L0_tok_kernel, L0_tok_scale, L0_tok_bias)
    h = h + _L0_attn_ref(_layernorm(h, axis=-1), L0_attn_Wq, L0_attn_Wk, L0_attn_Wv)
    h = h + _L0_ffn_ref(_layernorm(h, axis=-1), L0_ffn_attention_mask, L0_ffn_wr, L0_ffn_br, L0_ffn_w1, L0_ffn_b1, L0_ffn_w2, L0_ffn_b2)
    h = h + _L1_attn_ref(_layernorm(h, axis=-1), L1_attn_E, L1_attn_Dx, L1_attn_Dy)
    h = h + _L1_ffn_ref(_layernorm(h, axis=-1), L1_ffn_Wr, L1_ffn_br, L1_ffn_ln_g, L1_ffn_ln_b, L1_ffn_W1, L1_ffn_b1, L1_ffn_W2, L1_ffn_b2)
    return h

_drawn_inputs = setup_inputs


def setup_inputs(seed=0):
    import zlib

    import numpy as np

    out = dict(_drawn_inputs(seed))
    spreads = {'L0_tok_bias': (0.0, 0.1),
     'L0_ffn_b1': (0.0, 0.8),
     'L0_ffn_b2': (0.0, 0.382),
     'L1_ffn_br': (0.0, 0.1),
     'L1_ffn_ln_g': (1.0, 0.2),
     'L1_ffn_ln_b': (0.0, 0.326),
     'L1_ffn_b1': (0.0, 0.335),
     'L1_ffn_b2': (0.0, 0.1)}
    factors = {'L0_ffn_wr': 3.641, 'L0_ffn_w1': 6.616, 'L0_ffn_w2': 7.288}
    for name, (base, spread) in spreads.items():
        noise = np.random.default_rng([zlib.crc32(name.encode()), seed]).standard_normal(out[name].shape)
        drawn = base * np.exp(spread * noise) if base else spread * noise
        out[name] = jnp.asarray(drawn.astype(out[name].dtype))
    for name, factor in factors.items():
        out[name] = (out[name] * factor).astype(out[name].dtype)
    return out
```

```python
import numpy as np

import concourse.bass as bass
from concourse import mybir
from contextlib import ExitStack

B, L, CIN, KW, D = 8, 375, 128, 15, 64
T = L - KW + 1
TP, NT = 121, 3
TT = TP * NT
XC = 2 * (KW // 2) + TT + 1
XP, XJ = 125, 3
G = 2
NP = B // G
Q = G * NT
H = 256
HC = H // 128
EXP, TOPK = 8, 2
KEEP = max(1, T // 2) - 1
DECAY = 0.97
TAPS = (KW + 1) // 2
UNITS = EXP * G
NEG = -1.0e10
TINY = float(np.finfo(np.float32).tiny)
SW = [T, 2 * TP, T]


def fields():
    groups = [
        [("conv", 2 * TAPS * D, CIN), ("eye2", D, 128), ("band", XJ * TT, XP), ("cbias", D, 128),
         ("cscale", 1, 128)],
        [("ident", 128, 128), ("wq", D, D), ("wk", D, D), ("wvT", D, D), ("smask", sum(SW), TP),
         ("wrB", TP, D), ("brB", 1, 128)],
        [("rankc", NT * T, TP), ("fw1", H, D), ("fb1", HC, 128), ("fw2", HC * D, 128), ("fb2", D, 128),
         ("dxT", H, D), ("ones", 128, 128), ("decay", 2 * TT, TP), ("dyT", H, D), ("eT", HC * D, 128),
         ("rw", EXP, D), ("rb", EXP, 128), ("topc", EXP * EXP, 128), ("eb2", D, EXP)],
        [("w1", EXP * H, D), ("gT", EXP, D), ("bT", EXP, D), ("b1", EXP * HC, 128),
         ("w2", EXP * HC * D, 128)],
    ]
    at = {}
    for n, group in enumerate(groups):
        c = 0
        for name, cols, rows in group:
            at[name] = (n, c, cols, rows)
            c += cols
    return at, [sum(g[1] for g in group) for group in groups]


def build(nc, x_nat, x_T, packs, out):
    f32 = mybir.dt.float32
    ALU = mybir.AluOpType
    ACT = mybir.ActivationFunctionType
    AX = mybir.AxisListType
    at, widths = fields()

    ctx = ExitStack()
    with ctx:
        def sb(name, shape):
            return ctx.enter_context(nc.sbuf_tensor(name, shape, f32))

        def sem(name):
            return ctx.enter_context(nc.semaphore(name))

        pack_sb = [sb(f"pack{n}", [128, w]) for n, w in enumerate(widths)]

        def field(name):
            n, c, cols, rows = at[name]
            return pack_sb[n][0:rows, c:c + cols]

        conv_w, eye2, cbias, cscale = field("conv"), field("eye2"), field("cbias"), field("cscale")
        band = field("band").rearrange("p (j t) -> p j t", j=XJ)
        ident, wq, wk, wvT, smask = (field(n) for n in ("ident", "wq", "wk", "wvT", "smask"))
        wrB, brB = field("wrB"), field("brB")
        rankc = field("rankc").rearrange("p (i t) -> p i t", i=NT)
        fw1, fb1, fb2 = field("fw1"), field("fb1"), field("fb2")
        fw2 = field("fw2").rearrange("p (c f) -> p c f", c=HC)
        dxT, dyT, ones, decay = field("dxT"), field("dyT"), field("ones"), field("decay")
        eT = field("eT").rearrange("p (c f) -> p c f", c=HC)
        rw, rb, eb2 = field("rw"), field("rb"), field("eb2")
        topc = field("topc").rearrange("p (e f) -> p e f", e=EXP)
        w1 = field("w1").rearrange("p (e n) -> p e n", e=EXP)
        gT, bT, b1 = field("gT"), field("bT"), field("b1")
        w2 = field("w2").rearrange("p (u f) -> p u f", f=D)

        wqk = sb("wqk", [D, D])
        w1g = sb("w1g", [D, EXP, H])
        b1f = sb("b1f", [128, EXP * HC])
        mhalf = sb("mhalf", [128, Q])

        xnat = sb("xnat", [XP, G, XJ, CIN])
        squares = sb("squares", [XP, G * XJ, CIN])
        sq = sb("sq", [XP, G * XJ])
        wn = sb("wn", [TP, Q])
        wr = sb("wr", [TP, Q])
        cs_scale = sb("cs_scale", [TP, Q])
        res = [sb(f"res{n}", [TP, Q, D]) for n in range(4)]
        xn = [sb(f"xn{n}", [TP, Q, D]) for n in range(8)]
        stats = [sb(f"stats{n}", [TP, Q, 6]) for n in range(8)]
        mv = [sb(f"mv{n}", [TP, Q, 2]) for n in range(8)]
        ve = [sb(f"ve{n}", [TP, Q]) for n in range(8)]
        rstd = [sb(f"rstd{n}", [TP, Q]) for n in range(8)]
        probs = sb("probs", [TP, Q, TT])
        smax = sb("smax", [TP, Q])
        nmax = sb("nmax", [TP, Q])
        ssum = sb("ssum", [TP, Q])
        rsum = sb("rsum", [TP, Q])
        vv = sb("vv", [TP, Q, D])
        wB = sb("wB", [TP, G, T])
        ranks = sb("ranks", [TP, Q, T])
        diags = sb("diags", [TP, 2, Q, TP])
        wcol = sb("wcol", [TP, Q])
        rank = sb("rank", [TP, Q])
        mw = sb("mw", [TP, Q])
        hx = sb("hx", [TP, Q, D])
        fy = sb("fy", [TP, Q, D])
        rt = sb("rt", [TP, Q])
        rsq = sb("rsq", [TP, Q])
        vra = sb("vra", [TP, Q])
        vrb = sb("vrb", [TP, Q])
        lnvr = sb("lnvr", [TP, Q, D])
        gd = sb("gd", [TP, G, 2 * TT])
        vstar = sb("vstar", [TP, Q, D])
        lg = sb("lg", [TP, Q, EXP])
        lmax = sb("lmax", [TP, Q])
        ex = sb("ex", [TP, Q, EXP])
        dif = sb("dif", [TP, Q, EXP, EXP])
        erank = sb("erank", [TP, Q, EXP])
        esel = sb("esel", [TP, Q, EXP])
        eden = sb("eden", [TP, Q])
        xT = sb("xT", [CIN, G, XC])
        cs = sb("cs", [128, G, TT])
        xnT = sb("xnT", [D, G, TT])
        gq = sb("gq", [D, G, TT])
        x2T = sb("x2T", [D, G, TT])
        hT = sb("hT", [128, G, HC, TT])
        vT = sb("vT", [D, G, TT])
        u = sb("u", [128, G, HC, TT])
        us = sb("us", [128, G, TT])
        ub = sb("ub", [128, G, TT])
        grown = sb("grown", [128, G, TT + 1])
        seen = sb("seen", [128, G, TT + 4])
        grow = sb("grow", [128, G, TT])
        den = sb("den", [128, G, TT])
        carry = sb("carry", [128, G, TT + 1])
        z = sb("z", [128, G, HC, TT])
        naT = sb("naT", [D, G, TT])
        yT = sb("yT", [128, G, HC, TT])
        x4T = sb("x4T", [D, G, TT])
        wT = sb("wT", [EXP, G, TT])
        x5T = sb("x5T", [D, G, TT])
        gate = sb("gate", [TP, Q, EXP])
        acc = sb("acc", [TP, Q, D])
        hid = sb("hid", [128, 2, HC, TT])
        outb = sb("outb", [TP, Q, D])

        FA = [ctx.enter_context(nc.psum_tensor(f"FA{h}", [128, 512], f32)) for h in range(G)]
        FB = [ctx.enter_context(nc.psum_tensor(f"FB{h}", [128, 512], f32)) for h in range(G)]
        HB = [ctx.enter_context(nc.psum_tensor(f"HB{h}", [128, 512], f32)) for h in range(HC)]
        YB = [ctx.enter_context(nc.psum_tensor(f"YB{h}", [128, 512], f32)) for h in range(2)]

        x_in, pack_in, out_st = sem("x_in"), [sem(f"pack_in{n}") for n in range(len(widths))], sem("out_st")
        out_free = sem("out_free")
        cst_set, wqk_mm, wqk_set, w1g_set, b1f_mm, b1f_set = (sem(n) for n in (
            "cst_set", "wqk_mm", "wqk_set", "w1g_set", "b1f_mm", "b1f_set"))
        pe = {n: sem("pe_" + n) for n in (
            "conv", "comb", "win", "t1", "proj", "sA", "v", "s2", "pv", "t2", "rt", "f1", "f2", "t3", "dx",
            "usum", "gram", "a", "t4", "dy", "e", "t5a", "t5b", "lg", "wt", "wb", "w1", "y")}
        ac = {n: sem("act_" + n) for n in (
            "sq", "cslo", "xnT", "gq", "exp", "x2T", "hT", "vT", "u", "us", "naT", "x4T", "x5T", "ex", "wT",
            "hid")}
        ve_s = {n: sem("dve_" + n) for n in (
            "cshi", "wn", "res0", "scA", "sc2", "nmax", "rsum", "vv", "res1", "wB", "wcol", "rank", "mw", "fy",
            "res2", "seen", "grow", "fed", "grown", "den", "guard", "carry", "z", "rt", "rsq", "gd", "yT", "lg", "lmax", "lsub",
            "dif", "cmp", "erank", "esel", "eden", "erec", "gate", "acc0", "acc")}
        po = {n: sem("pool_" + n) for n in ("wr", "scale", "hx", "ub", "lnvr", "var_a", "res3")}
        ln_st = [sem(f"ln_st{n}") for n in range(8)]
        ln_mv = [sem(f"ln_mv{n}") for n in range(8)]
        ln_ve = [sem(f"ln_ve{n}") for n in range(8)]
        ln_rs = [sem(f"ln_rs{n}") for n in range(8)]
        ln_xn = [sem(f"ln_xn{n}") for n in range(8)]
        LN_EPS = 1e-5

        block = ctx.enter_context(nc.Block())

        def tile_q(h, i):
            return NT * h + i

        @block.sync
        def _(sp):
            def load_x(pair, later=True):
                if later:
                    sp.wait_ge(pe["conv"], G * pair)
                    sp.wait_ge(ac["sq"], pair)
                sp.dma_start(xT[:, :, :], x_T[:, bass.ds(pair * G, G), :]).then_inc(x_in, 16)
                sp.dma_start(xnat[:, :, :, :], x_nat[:, bass.ds(pair * G, G), :, :]).then_inc(x_in, 16)

            def store(pair):
                sp.wait_ge(ve_s["acc"], UNITS * pair + UNITS)
                sp.dma_start(out[:, bass.ds(pair * Q, Q), :], outb[:, :, :]).then_inc(out_st, 16)
                sp.wait_ge(out_st, 16 * pair + 16)
                sp.sem_inc(out_free, 1)

            sp.dma_start(pack_sb[0][:, :], packs[0]).then_inc(pack_in[0], 16)
            sp.sem_inc(out_free, 1)
            load_x(0, later=False)
            for n in range(1, len(widths)):
                sp.dma_start(pack_sb[n][:, :], packs[n]).then_inc(pack_in[n], 16)
            load_x(1)
            with sp.Fori(0, NP - 2) as pair:
                load_x(pair + 2)
                store(pair)
            store(NP - 2)
            store(NP - 1)

        @block.tensor
        def _(te):
            mm = nc.tensor.matmul

            def tok(i):
                return slice(TP * i, TP * (i + 1))

            def transposes(dst, src, h, done):
                te.nop(nofuse=True)
                for i in range(NT):
                    last = nc.tensor.transpose(dst[0:D, tok(i)], src[:, tile_q(h, i), :], ident[0:TP, 0:TP])
                last.then_inc(done, 1)

            def to_hidden(w, src, h, c, dst):
                return mm(dst[:, 0:TT], w[:, 128 * c:128 * (c + 1)], src[:, h, :], start=True, stop=True)

            def from_hidden(src, w, dst):
                for i in range(NT):
                    for c in range(HC):
                        last = mm(dst[0:TP, D * i:D * (i + 1)], src[:, c, tok(i)], w[:, c, :],
                                  start=(c == 0), stop=(c == HC - 1))
                return last

            def conv(pair):
                te.wait_ge(x_in, 32 * (pair + 1))
                if not (isinstance(pair, int) and pair == 0):
                    te.wait_ge(ve_s["acc0"], G * pair)
                for h in range(G):
                    for k in range(TAPS):
                        last = mm(FB[h][:, 0:TT + 1], conv_w[:, 2 * D * k:2 * D * (k + 1)],
                                  xT[:, h, 2 * k:2 * k + TT + 1], start=(k == 0), stop=(k == TAPS - 1))
                    last.then_inc(pe["conv"], 1)

            def combine(pair):
                for h in range(G):
                    te.wait_ge(ac["cslo"], G * pair + h + 1)
                    te.wait_ge(ve_s["cshi"], G * pair + h + 1)
                    for i in range(NT):
                        last = mm(FA[h][0:TP, D * i:D * (i + 1)], cs[:, h, tok(i)], eye2, start=True, stop=True)
                    last.then_inc(pe["comb"], 1)
                te.wait_ge(ac["sq"], pair + 1)
                for i in range(NT):
                    for j in range(XJ):
                        last = mm(FB[0][0:TP, G * i:G * (i + 1)], band[:, j, tok(i)], sq[:, j::XJ],
                                  start=(j == 0), stop=(j == XJ - 1))
                last.then_inc(pe["win"], 1)

            def t1(pair):
                for h in range(G):
                    te.wait_ge(ln_xn[0], G * pair + h + 1)
                    transposes(FA[h], xn[0], h, pe["t1"])

            def proj(pair):
                for h in range(G):
                    te.wait_ge(ac["xnT"], G * pair + h + 1)
                    te.nop(nofuse=True)
                    mm(FB[h][0:D, 0:TT], wqk[:, :], xnT[:, h, :], start=True, stop=True).then_inc(pe["proj"], 1)

            def scores_a(pair):
                for h in range(G):
                    te.wait_ge(ac["gq"], G * pair + h + 1)
                    for n, bank in enumerate((FA[h], FB[h])):
                        mm(bank[0:TP, 0:SW[n]], xnT[:, h, tok(n)], gq[:, h, 0:SW[n]],
                           start=True, stop=True).then_inc(pe["sA"], 1)

            def scores_b(pair):
                for h in range(G):
                    te.wait_ge(ve_s["scA"], 2 * (G * pair + h) + 2)
                    mm(FB[h][0:TP, 0:SW[2]], xnT[:, h, tok(2)], gq[:, h, 0:SW[2]],
                       start=True, stop=True).then_inc(pe["s2"], 1)
                    for i in range(NT):
                        last = mm(FA[h][0:TP, D * i:D * (i + 1)], xnT[:, h, tok(i)], wvT, start=True, stop=True)
                    last.then_inc(pe["v"], 1)

            def pv(pair):
                for h in range(G):
                    te.wait_ge(ve_s["vv"], G * pair + h + 1)
                    for i in range(NT):
                        keys = [0, 1, 2] if i < 2 else [0, 2]
                        for k in keys:
                            rows = min(TP, T - TP * k)
                            last = mm(FB[h][0:TP, D * i:D * (i + 1)], probs[0:rows, tile_q(h, k), tok(i)],
                                      vv[0:rows, tile_q(h, k), :], start=(k == 0), stop=(k == keys[-1]))
                    last.then_inc(pe["pv"], 1)

            def t2(pair):
                for h in range(G):
                    te.wait_ge(ln_xn[1], G * pair + h + 1)
                    transposes(FA[h], xn[1], h, pe["t2"])

            def router(pair):
                for h in range(G):
                    te.wait_ge(ac["x2T"], G * pair + h + 1)
                    mm(FB[h][0:TP, 0:T], wrB, x2T[:, h, 0:T], start=True, stop=True).then_inc(pe["rt"], 1)

            def ffn_up(pair):
                for h in range(G):
                    to_hidden(fw1, x2T, h, 0, FA[h]).then_inc(pe["f1"], 1)
                for h in range(G):
                    te.wait_ge(ve_s["wB"], G * pair + h + 1)
                    to_hidden(fw1, x2T, h, 1, FB[h]).then_inc(pe["f1"], 1)

            def ffn_down(pair):
                for h in range(G):
                    te.wait_ge(ac["hT"], HC * G * pair + G + h + 1)
                    from_hidden(hT[:, h, :, :], fw2, FA[h]).then_inc(pe["f2"], 1)

            def t3(pair):
                for h in range(G):
                    te.wait_ge(ln_xn[2], G * pair + h + 1)
                    transposes(FB[h], xn[2], h, pe["t3"])

            def dx(pair):
                for h in range(G):
                    te.wait_ge(ac["vT"], G * pair + h + 1)
                    to_hidden(dxT, vT, h, 0, FA[h]).then_inc(pe["dx"], 1)
                for h in range(G):
                    to_hidden(dxT, vT, h, 1, FB[h]).then_inc(pe["dx"], 1)

            def usum(pair):
                for h in range(G):
                    te.wait_ge(ac["u"], HC * G * pair + G + h + 1)
                    for c in range(HC):
                        last = mm(FA[h][:, 0:TT], ones, u[:, h, c, :], start=(c == 0), stop=(c == HC - 1))
                    last.then_inc(pe["usum"], 1)

            def gram(pair):
                for h in range(G):
                    te.wait_ge(ve_s["z"], G * pair + h + 1)
                    for bank, tiles in ((FA[h], (0,)), (FB[h], (1, 2))):
                        at_col = 0
                        for i in tiles:
                            w = TT - TP * i
                            for c in range(HC):
                                last = mm(bank[0:TP, at_col:at_col + w], z[:, h, c, tok(i)],
                                          z[:, h, c, TP * i:TT], start=(c == 0), stop=(c == HC - 1))
                            at_col += w
                        last.then_inc(pe["gram"], 1)

            def linear(pair):
                te.wait_ge(po["lnvr"], pair + 1)
                for h in range(G):
                    te.wait_ge(ve_s["gd"], 2 * (G * pair + h) + 2)
                    for k in range(NT):
                        for i in range(k + 1):
                            first = (0, TT, TT + 2 * TP)[i] + TP * (k - i)
                            last = mm(FA[h][0:TP, D * k:D * (k + 1)], gd[:, h, first:first + TP],
                                      lnvr[:, tile_q(h, i), :], start=(i == 0), stop=(i == k))
                    last.then_inc(pe["a"], 1)

            def t4(pair):
                for h in range(G):
                    te.wait_ge(ln_xn[4], G * pair + h + 1)
                    transposes(FB[h], xn[4], h, pe["t4"])

            def dy(pair):
                for h in range(G):
                    te.wait_ge(ac["naT"], G * pair + h + 1)
                    to_hidden(dyT, naT, h, 0, FA[h]).then_inc(pe["dy"], 1)
                for h in range(G):
                    to_hidden(dyT, naT, h, 1, FB[h]).then_inc(pe["dy"], 1)

            def embed(pair):
                for h in range(G):
                    te.wait_ge(ve_s["yT"], HC * G * pair + G + h + 1)
                    from_hidden(yT[:, h, :, :], eT, FA[h]).then_inc(pe["e"], 1)

            def t5(pair):
                for h in range(G):
                    te.wait_ge(ln_xn[6], G * pair + h + 1)
                    transposes(FB[h], xn[6], h, pe["t5a"])
                for h in range(G):
                    te.wait_ge(ln_xn[7], G * pair + h + 1)
                    transposes(FA[h], xn[7], h, pe["t5b"])

            def route(pair):
                for h in range(G):
                    te.wait_ge(ac["x4T"], G * pair + h + 1)
                    for i in range(NT):
                        last = mm(FB[h][0:TP, EXP * i:EXP * (i + 1)], x4T[:, h, tok(i)], rw, start=True, stop=True)
                    last.then_inc(pe["lg"], 1)
                te.wait_ge(ve_s["gate"], pair + 1)
                for h in range(G):
                    for i in range(NT):
                        last = nc.tensor.transpose(FB[h][0:EXP, tok(i)], gate[:, tile_q(h, i), :],
                                                   ident[0:TP, 0:TP])
                    last.then_inc(pe["wt"], 1)
                te.wait_ge(ac["x5T"], G * pair + G)
                for h in range(G):
                    te.wait_ge(ac["wT"], G * pair + h + 1)
                    for i in range(NT):
                        last = mm(FA[h][0:TP, D * i:D * (i + 1)], wT[:, h, tok(i)], eb2, start=True, stop=True)
                    last.then_inc(pe["wb"], 1)

            def up(pair, n):
                e, h = n // G, n % G
                for c in range(HC):
                    if n:
                        te.wait_ge(ac["hid"], HC * (UNITS * pair + n - 1) + c + 1)
                    to_hidden(w1g[:, e, :], x5T, h, c, HB[c]).then_inc(pe["w1"], 1)

            def down(pair, n):
                te.wait_ge(ac["hid"], HC * (UNITS * pair + n) + HC)
                if n >= 2:
                    te.wait_ge(ve_s["acc"], UNITS * pair + n - 1)
                from_hidden(hid[:, n % 2, :, :], w2[:, HC * (n // G):HC * (n // G + 1), :],
                            YB[n % 2]).then_inc(pe["y"], 1)

            front = [conv, combine, t1, proj, scores_a, scores_b, pv, t2, router, ffn_up, ffn_down, t3, dx,
                     usum, gram, linear, t4, dy, embed, t5, route]

            def experts(pair, n):
                if n < UNITS:
                    up(pair, n)
                if 0 < n <= UNITS:
                    down(pair, n - 1)

            te.wait_ge(pack_in[0], 16)
            conv(0)
            te.wait_ge(pack_in[1], 16)
            mm(HB[0][0:D, 0:D], wq, wk, start=True, stop=True).then_inc(wqk_mm, 1)
            combine(0)
            t1(0)
            te.wait_ge(wqk_set, 1)
            te.wait_ge(pack_in[2], 16)
            te.wait_ge(pack_in[3], 16)
            for n in range(EXP * HC):
                e, c = n // HC, n % HC
                last = mm(HB[1][:, n:n + 1], w1[:, e, 128 * c:128 * (c + 1)], bT[:, e:e + 1], start=True, stop=True)
            last.then_inc(b1f_mm, 1)
            for stage in front[3:]:
                stage(0)
            te.wait_ge(w1g_set, 1)
            te.wait_ge(b1f_set, 1)
            with te.Fori(0, NP - 1) as pair:
                te.wait_ge(ac["x5T"], G * pair + G)
                for n, stage in enumerate(front):
                    stage(pair + 1)
                    experts(pair, n)
            for n in range(UNITS + 1):
                experts(NP - 1, n)

        @block.scalar
        def _(se):
            act = nc.scalar.activation

            def from_bank(dst, bank, h, pair, produced, done):
                se.wait_ge(produced, G * pair + h + 1)
                act(dst[:, h, :], bank[h][0:D, 0:TT], ACT.Copy).then_inc(done, 1)

            def conv(pair):
                se.wait_ge(x_in, 32 * (pair + 1))
                for h in range(G):
                    for j in range(XJ):
                        last = act(squares[:, XJ * h + j, :], xnat[:, h, j, :], ACT.Square,
                                   accum_out=sq[:, XJ * h + j:XJ * h + j + 1])
                last.then_inc(ac["sq"], 1)
                for h in range(G):
                    se.wait_ge(pe["conv"], G * pair + h + 1)
                    act(cs[0:D, h, :], FB[h][0:D, 0:TT], ACT.Copy).then_inc(ac["cslo"], 1)

            def t1(pair):
                for h in range(G):
                    from_bank(xnT, FA, h, pair, pe["t1"], ac["xnT"])

            def proj(pair):
                for h in range(G):
                    from_bank(gq, FB, h, pair, pe["proj"], ac["gq"])

            def scores_b(pair):
                se.wait_ge(ve_s["nmax"], pair + 1)
                for h in range(G):
                    for i in range(NT):
                        q = tile_q(h, i)
                        last = act(probs[:, q, 0:SW[i]], probs[:, q, 0:SW[i]], ACT.Exp, bias=nmax[:, q:q + 1],
                                   accum_out=ssum[:, q:q + 1])
                    last.then_inc(ac["exp"], 1)

            def t2(pair):
                for h in range(G):
                    from_bank(x2T, FA, h, pair, pe["t2"], ac["x2T"])

            def ffn_up(pair):
                for n in range(HC * G):
                    c, h = n // G, n % G
                    se.wait_ge(pe["f1"], HC * G * pair + n + 1)
                    act(hT[:, h, c, :], (FA, FB)[c][h][:, 0:TT], ACT.Gelu_apprx_tanh,
                        bias=fb1[:, c:c + 1]).then_inc(ac["hT"], 1)

            def t3(pair):
                for h in range(G):
                    from_bank(vT, FB, h, pair, pe["t3"], ac["vT"])

            def dx(pair):
                for n in range(HC * G):
                    c, h = n // G, n % G
                    se.wait_ge(pe["dx"], HC * G * pair + n + 1)
                    act(u[:, h, c, :], (FA, FB)[c][h][:, 0:TT], ACT.Relu).then_inc(ac["u"], 1)

            def usum(pair):
                for h in range(G):
                    se.wait_ge(pe["usum"], G * pair + h + 1)
                    act(us[:, h, :], FA[h][:, 0:TT], ACT.Copy, scale=1.0 / DECAY).then_inc(ac["us"], 1)

            def t4(pair):
                for h in range(G):
                    from_bank(naT, FB, h, pair, pe["t4"], ac["naT"])

            def t5(pair):
                for h in range(G):
                    from_bank(x4T, FB, h, pair, pe["t5a"], ac["x4T"])
                for h in range(G):
                    from_bank(x5T, FA, h, pair, pe["t5b"], ac["x5T"])

            def route(pair):
                se.wait_ge(ve_s["lsub"], pair + 1)
                act(ex[:, :, :], lg[:, :, :], ACT.Exp).then_inc(ac["ex"], 1)
                for h in range(G):
                    se.wait_ge(pe["wt"], G * pair + h + 1)
                    act(wT[:, h, :], FB[h][0:EXP, 0:TT], ACT.Copy).then_inc(ac["wT"], 1)

            def experts(pair, n):
                if n >= UNITS:
                    return
                e = n // G
                if n >= 2:
                    se.wait_ge(pe["y"], UNITS * pair + n - 1)
                for c in range(HC):
                    se.wait_ge(pe["w1"], HC * (UNITS * pair + n) + c + 1)
                    act(hid[:, n % 2, c, :], HB[c][:, 0:TT], ACT.Gelu,
                        bias=b1f[:, HC * e + c:HC * e + c + 1]).then_inc(ac["hid"], 1)

            def none(pair):
                pass

            front = [conv, none, t1, proj, none, scores_b, none, t2, none, ffn_up, none, t3, dx,
                     usum, none, none, t4, none, none, t5, route]
            conv(0)
            se.wait_ge(wqk_mm, 1)
            act(wqk[:, :], HB[0][0:D, 0:D], ACT.Copy).then_inc(wqk_set, 1)
            for stage in front[1:]:
                if stage is ffn_up:
                    se.wait_ge(pack_in[2], 16)
                stage(0)
            se.wait_ge(b1f_set, 1)
            with se.Fori(0, NP - 1) as pair:
                for n, stage in enumerate(front):
                    stage(pair + 1)
                    experts(pair, n)
            for n in range(UNITS):
                experts(NP - 1, n)

        @block.vector
        def _(dv):
            V = nc.vector

            def each(ap):
                return ap.unsqueeze(2).to_broadcast([TP, ap.shape[1], D])

            def ln_stats(n, source, pair):
                for q in range(Q):
                    last = V.bn_stats(stats[n][:, q, :], source(q))
                last.then_inc(ln_st[n], 1)
                dv.wait_ge(ln_st[n], pair + 1)
                dv.nop(nofuse=True)
                for q in range(Q):
                    last = V.bn_aggr(mv[n][:, q, :], stats[n][:, q, :])
                last.then_inc(ln_mv[n], 1)

            def ln_apply(n, source, pair, dst):
                dv.wait_ge(ln_rs[n], pair + 1)
                for q in range(Q):
                    last = V.tensor_scalar(dst[:, q, :], source(q), mv[n][:, q, 0:1], rstd[n][:, q:q + 1],
                                           ALU.subtract, ALU.mult)
                    if q % NT == NT - 1:
                        last.then_inc(ln_xn[n], 1)

            def layernorm(n, src, pair):
                ln_stats(n, lambda q: src[:, q, :], pair)
                ln_apply(n, lambda q: src[:, q, :], pair, xn[n])

            def in_bank(bank):
                return lambda q: bank[q // NT][0:TP, D * (q % NT):D * (q % NT + 1)]

            def conv(pair):
                for h in range(G):
                    dv.wait_ge(pe["conv"], G * pair + h + 1)
                    V.tensor_copy(cs[D:128, h, :], FB[h][D:128, 1:TT + 1]).then_inc(ve_s["cshi"], 1)

            def combine(pair):
                dv.wait_ge(pe["win"], pair + 1)
                V.tensor_scalar(wn[:, :].rearrange("p (h i) -> p i h", h=G),
                                FB[0][0:TP, 0:Q].rearrange("p (i h) -> p i h", h=G),
                                1e-7, None, ALU.add).then_inc(ve_s["wn"], 1)
                dv.wait_ge(po["scale"], pair + 1)
                dv.wait_ge(pe["comb"], G * pair + G)
                for q in range(Q):
                    last = V.scalar_tensor_tensor(res[0][:, q, :], in_bank(FA)(q), cs_scale[:, q:q + 1],
                                                  cbias[0:TP, :], ALU.mult, ALU.add)
                last.then_inc(ve_s["res0"], 1)
                dv.wait_ge(ve_s["res0"], pair + 1)
                layernorm(0, res[0], pair)

            def score_tile(h, n, bank, done):
                q = tile_q(h, n)
                V.tensor_tensor_reduce(out=probs[:, q, 0:SW[n]], in0=bank[0:TP, 0:SW[n]],
                                       in1=smask[:, sum(SW[:n]):sum(SW[:n + 1])], scale=D ** -0.5,
                                       scalar=-3.0e38, op0=ALU.add, op1=ALU.max,
                                       accum_out=smax[:, q:q + 1]).then_inc(done, 1)

            def scores_a(pair):
                for h in range(G):
                    for n, bank in enumerate((FA[h], FB[h])):
                        dv.wait_ge(pe["sA"], 2 * (G * pair + h) + n + 1)
                        dv.nop(nofuse=True)
                        score_tile(h, n, bank, ve_s["scA"])

            def scores_b(pair):
                for h in range(G):
                    dv.wait_ge(pe["s2"], G * pair + h + 1)
                    dv.nop(nofuse=True)
                    score_tile(h, 2, FB[h], ve_s["sc2"])
                dv.wait_ge(ve_s["sc2"], G * pair + G)
                V.tensor_scalar(nmax[:, :], smax[:, :], -1.0, None, ALU.mult).then_inc(ve_s["nmax"], 1)
                dv.wait_ge(ac["exp"], G * pair + G)
                V.reciprocal(rsum[:, :], ssum[:, :]).then_inc(ve_s["rsum"], 1)
                dv.wait_ge(ve_s["rsum"], pair + 1)
                for h in range(G):
                    dv.wait_ge(pe["v"], G * pair + h + 1)
                    V.tensor_tensor(vv[:, NT * h:NT * (h + 1), :],
                                    FA[h][0:TP, 0:NT * D].rearrange("p (i f) -> p i f", i=NT),
                                    each(rsum[:, NT * h:NT * (h + 1)]), ALU.mult).then_inc(ve_s["vv"], 1)

            def pv(pair):
                for h in range(G):
                    dv.wait_ge(pe["pv"], G * pair + h + 1)
                    V.tensor_tensor(res[1][:, NT * h:NT * (h + 1), :],
                                    FB[h][0:TP, 0:NT * D].rearrange("p (i f) -> p i f", i=NT),
                                    res[0][:, NT * h:NT * (h + 1), :], ALU.add).then_inc(ve_s["res1"], 1)
                dv.wait_ge(ve_s["res1"], G * pair + G)
                layernorm(1, res[1], pair)

            def diagonal(dst, row, h, scale, n):
                for i in range(NT):
                    w = min(TP, row.shape[1] - TP * i)
                    last = V.tensor_tensor_reduce(out=diags[:, n, tile_q(h, i), 0:w], in0=row[:, TP * i:TP * i + w],
                                                  in1=ident[0:TP, 0:w], scale=scale, scalar=0.0, op0=ALU.mult,
                                                  op1=ALU.add, accum_out=dst[:, tile_q(h, i):tile_q(h, i) + 1])
                return last

            def router(pair):
                for h in range(G):
                    dv.wait_ge(pe["rt"], G * pair + h + 1)
                    V.tensor_scalar(wB[:, h, :], FB[h][0:TP, 0:T], brB[0:TP, 0:1], None,
                                    ALU.add).then_inc(ve_s["wB"], 1)
                dv.wait_ge(ve_s["wB"], G * pair + G)
                for h in range(G):
                    last = diagonal(wcol, wB[:, h, :], h, 1.0, 0)
                last.then_inc(ve_s["wcol"], 1)
                dv.wait_ge(ve_s["wcol"], pair + 1)
                for h in range(G):
                    for i in range(NT):
                        q = tile_q(h, i)
                        last = V.scalar_tensor_tensor(ranks[:, q, :], wB[:, h, :], wcol[:, q:q + 1], rankc[:, i, :],
                                                      ALU.subtract, ALU.is_ge, accum_out=rank[:, q:q + 1])
                last.then_inc(ve_s["rank"], 1)
                dv.wait_ge(ve_s["rank"], pair + 1)
                V.scalar_tensor_tensor(mw[:, :], rank[:, :], float(KEEP), wcol[:, :], ALU.is_lt,
                                       ALU.mult).then_inc(ve_s["mw"], 1)

            def ffn_down(pair):
                for h in range(G):
                    dv.wait_ge(pe["f2"], G * pair + h + 1)
                    V.tensor_tensor(fy[:, NT * h:NT * (h + 1), :],
                                    FA[h][0:TP, 0:NT * D].rearrange("p (i f) -> p i f", i=NT),
                                    fb2[0:TP, :].unsqueeze(1).to_broadcast([TP, NT, D]),
                                    ALU.add).then_inc(ve_s["fy"], 1)
                dv.wait_ge(ve_s["fy"], G * pair + G)
                dv.wait_ge(ve_s["mw"], pair + 1)
                dv.wait_ge(po["hx"], pair + 1)
                for q in range(Q):
                    last = V.scalar_tensor_tensor(res[2][:, q, :], fy[:, q, :], mw[:, q:q + 1], hx[:, q, :],
                                                  ALU.mult, ALU.add)
                last.then_inc(ve_s["res2"], 1)
                dv.wait_ge(ve_s["res2"], pair + 1)
                layernorm(2, res[2], pair)
                dv.wait_ge(ln_xn[2], G * pair + G)
                layernorm(3, xn[2], pair)

            def usum(pair):
                for h in range(G):
                    dv.wait_ge(ac["us"], G * pair + h + 1)
                    V.tensor_tensor_scan(seen[:, h, 4:TT + 4], us[:, h, :], us[:, h, :], 0.0, ALU.max,
                                         ALU.max).then_inc(ve_s["seen"], 1)
                dv.wait_ge(ve_s["seen"], G * pair + G)
                V.tensor_scalar(grow[:, :, :], seen[:, :, 0:TT], 0.0, DECAY * 1e12, ALU.is_equal,
                                ALU.mult).then_inc(ve_s["grow"], 1)
                dv.wait_ge(po["ub"], G * pair + G)
                V.scalar_tensor_tensor(ub[:, :, :], seen[:, :, 1:TT + 1], 0.0, ub[:, :, :], ALU.is_gt,
                                       ALU.add).then_inc(ve_s["fed"], 1)
                dv.wait_ge(ve_s["grow"], pair + 1)
                dv.wait_ge(ve_s["fed"], pair + 1)
                for h in range(G):
                    V.tensor_tensor_scan(grown[:, h, 1:TT + 1], grow[:, h, :], ub[:, h, :], 0.0, ALU.mult,
                                         ALU.add).then_inc(ve_s["grown"], 1)
                dv.wait_ge(ve_s["grown"], G * pair + G)
                V.scalar_tensor_tensor(den[:, :, :], grown[:, :, 0:TT], 1.0, us[:, :, :], ALU.min,
                                       ALU.add).then_inc(ve_s["den"], 1)
                dv.wait_ge(ve_s["den"], pair + 1)
                V.tensor_scalar(den[:, :, :], den[:, :, :], 1e-12 / DECAY, None, ALU.max).then_inc(ve_s["guard"], 1)
                dv.wait_ge(ve_s["guard"], pair + 1)
                V.reciprocal(carry[:, :, 1:TT + 1], den[:, :, :]).then_inc(ve_s["carry"], 1)
                dv.wait_ge(ve_s["carry"], pair + 1)
                for h in range(G):
                    for c in range(HC):
                        last = V.tensor_tensor_scan(z[:, h, c, :], carry[:, h, 0:TT], u[:, h, c, :], 0.0,
                                                    ALU.mult, ALU.add)
                    last.then_inc(ve_s["z"], 1)
                for h in range(G):
                    last = diagonal(rt, carry[0:TP, h, 1:TT + 1], h, 1.0 / DECAY, 1)
                last.then_inc(ve_s["rt"], 1)
                dv.wait_ge(ve_s["rt"], pair + 1)
                V.tensor_tensor(rsq[:, :], rt[:, :], rt[:, :], ALU.mult).then_inc(ve_s["rsq"], 1)

            def gram(pair):
                for h in range(G):
                    for n, bank in enumerate((FA[h], FB[h])):
                        dv.wait_ge(pe["gram"], 2 * (G * pair + h) + n + 1)
                        V.tensor_tensor(gd[:, h, TT * n:TT * (n + 1)], bank[0:TP, 0:TT],
                                        decay[:, TT * n:TT * (n + 1)], ALU.mult).then_inc(ve_s["gd"], 1)

            def linear(pair):
                dv.wait_ge(pe["a"], G * pair + G)
                ln_stats(4, in_bank(FA), pair)
                ln_apply(4, in_bank(FA), pair, xn[4])

            def dy(pair):
                for n in range(HC * G):
                    c, h = n // G, n % G
                    dv.wait_ge(pe["dy"], HC * G * pair + n + 1)
                    V.scalar_tensor_tensor(yT[:, h, c, :], (FA, FB)[c][h][:, 0:TT], 0.0, z[:, h, c, :],
                                           ALU.max, ALU.mult).then_inc(ve_s["yT"], 1)

            def embed(pair):
                dv.wait_ge(pe["e"], G * pair + G)
                ln_stats(5, in_bank(FA), pair)
                ln_apply(5, in_bank(FA), pair, xn[5])
                dv.wait_ge(ln_xn[5], G * pair + G)
                V.tensor_tensor(res[3][:, :, :], xn[5][:, :, :], res[2][:, :, :], ALU.add).then_inc(po["res3"], 1)
                dv.wait_ge(po["res3"], pair + 1)
                layernorm(6, res[3], pair)
                dv.wait_ge(ln_xn[6], G * pair + G)
                layernorm(7, xn[6], pair)

            def per_expert(ap):
                return ap.unsqueeze(2).to_broadcast([TP, Q, EXP])

            def route(pair):
                for h in range(G):
                    dv.wait_ge(pe["lg"], G * pair + h + 1)
                    V.tensor_tensor(lg[:, NT * h:NT * (h + 1), :],
                                    FB[h][0:TP, 0:NT * EXP].rearrange("p (i e) -> p i e", i=NT),
                                    rb[0:TP, :].unsqueeze(1).to_broadcast([TP, NT, EXP]),
                                    ALU.add).then_inc(ve_s["lg"], 1)
                dv.wait_ge(ve_s["lg"], G * pair + G)
                V.reduce_max(lmax[:, :], lg[:, :, :], AX.X).then_inc(ve_s["lmax"], 1)
                dv.wait_ge(ve_s["lmax"], pair + 1)
                V.tensor_tensor(lg[:, :, :], lg[:, :, :], per_expert(lmax[:, :]),
                                ALU.subtract).then_inc(ve_s["lsub"], 1)
                dv.wait_ge(ac["ex"], pair + 1)
                V.tensor_tensor(dif[:, :, :, :], ex[:, :, :].unsqueeze(2).to_broadcast([TP, Q, EXP, EXP]),
                                ex[:, :, :].unsqueeze(3).to_broadcast([TP, Q, EXP, EXP]),
                                ALU.subtract).then_inc(ve_s["dif"], 1)
                dv.wait_ge(ve_s["dif"], pair + 1)
                V.tensor_tensor(dif[:, :, :, :], dif[:, :, :, :],
                                topc[0:TP, :, :].unsqueeze(1).to_broadcast([TP, Q, EXP, EXP]),
                                ALU.is_ge).then_inc(ve_s["cmp"], 1)
                dv.wait_ge(ve_s["cmp"], pair + 1)
                V.reduce_sum(erank[:, :, :], dif[:, :, :, :], AX.X).then_inc(ve_s["erank"], 1)
                dv.wait_ge(ve_s["erank"], pair + 1)
                V.scalar_tensor_tensor(esel[:, :, :], erank[:, :, :], float(TOPK), ex[:, :, :], ALU.is_lt,
                                       ALU.mult).then_inc(ve_s["esel"], 1)
                dv.wait_ge(ve_s["esel"], pair + 1)
                V.reduce_sum(eden[:, :], esel[:, :, :], AX.X).then_inc(ve_s["eden"], 1)
                dv.wait_ge(ve_s["eden"], pair + 1)
                V.reciprocal(eden[:, :], eden[:, :]).then_inc(ve_s["erec"], 1)
                dv.wait_ge(ve_s["erec"], pair + 1)
                V.tensor_tensor(gate[:, :, :], esel[:, :, :], per_expert(eden[:, :]),
                                ALU.mult).then_inc(ve_s["gate"], 1)
                for h in range(G):
                    dv.wait_ge(pe["wb"], G * pair + h + 1)
                    V.tensor_tensor(acc[:, NT * h:NT * (h + 1), :],
                                    FA[h][0:TP, 0:NT * D].rearrange("p (i f) -> p i f", i=NT),
                                    res[3][:, NT * h:NT * (h + 1), :], ALU.add).then_inc(ve_s["acc0"], 1)

            def experts(pair, n):
                n -= 1
                if not 0 <= n < UNITS:
                    return
                e, h = n // G, n % G
                dv.wait_ge(pe["y"], UNITS * pair + n + 1)
                if e == 0:
                    dv.wait_ge(ve_s["acc0"], G * pair + G)
                else:
                    dv.wait_ge(ve_s["acc"], UNITS * pair + n - 1)
                if e == EXP - 1:
                    dv.wait_ge(out_free, pair + 1)
                into = outb if e == EXP - 1 else acc
                for i in range(NT):
                    q = tile_q(h, i)
                    last = V.scalar_tensor_tensor(into[:, q, :], YB[n % 2][0:TP, D * i:D * (i + 1)],
                                                  gate[:, q, e:e + 1], acc[:, q, :], ALU.mult, ALU.add)
                last.then_inc(ve_s["acc"], 1)

            def none(pair):
                pass

            front = [conv, combine, none, none, scores_a, scores_b, pv, none, router, none, ffn_down, none, none,
                     usum, gram, linear, none, dy, embed, none, route]

            V.memset(mhalf[:, :], -0.5)
            V.memset(seen[:, :, 0:4], 0.0)
            V.memset(grown[:, :, 0:1], 0.0)
            V.memset(carry[:, :, 0:1], 0.0)
            V.memset(probs[:, :, T:TT], 0.0).then_inc(cst_set, 1)
            dv.wait_ge(pack_in[0], 16)
            conv(0)
            combine(0)
            dv.wait_ge(pack_in[1], 16)
            dv.wait_ge(cst_set, 1)
            for stage in front[2:7]:
                stage(0)
            dv.wait_ge(pack_in[2], 16)
            dv.wait_ge(pack_in[3], 16)
            V.tensor_tensor(w1g[:, :, :], w1, gT.unsqueeze(2).to_broadcast([D, EXP, H]),
                            ALU.mult).then_inc(w1g_set, 1)
            dv.wait_ge(b1f_mm, 1)
            V.tensor_tensor(b1f[:, :], HB[1][:, 0:EXP * HC], b1, ALU.add).then_inc(b1f_set, 1)
            for stage in front[7:]:
                stage(0)
            with dv.Fori(0, NP - 1) as pair:
                for n, stage in enumerate(front):
                    stage(pair + 1)
                    experts(pair, n)
            for n in range(UNITS + 1):
                experts(NP - 1, n)

        @block.gpsimd
        def _(gp):
            P = nc.gpsimd

            def root(n, pair):
                gp.wait_ge(ln_mv[n], pair + 1)
                gp.nop(nofuse=True)
                P.tensor_scalar(ve[n][:, :], mv[n][:, :, 1], LN_EPS, 1.0, ALU.add, ALU.mult).then_inc(ln_ve[n], 1)
                gp.wait_ge(ln_ve[n], pair + 1)
                P.tensor_tensor(rstd[n][:, :], ve[n][:, :], mhalf[0:TP, :], ALU.pow).then_inc(ln_rs[n], 1)

            def scaled_root(n, pair):
                gp.wait_ge(ln_mv[n], pair + 1)
                gp.wait_ge(ve_s["rsq"], pair + 1)
                P.tensor_tensor(ve[n][:, :], mv[n][:, :, 1], rsq[:, :], ALU.mult).then_inc(ln_ve[n], 1)
                gp.wait_ge(ln_ve[n], 3 * pair + 1)
                gp.nop(nofuse=True)
                P.tensor_scalar(vra[:, :], ve[n][:, :], LN_EPS, 1.0, ALU.add, ALU.mult).then_inc(ln_ve[n], 1)
                gp.wait_ge(ln_ve[n], 3 * pair + 2)
                P.tensor_tensor(vrb[:, :], vra[:, :], mhalf[0:TP, :], ALU.pow).then_inc(ln_ve[n], 1)
                gp.wait_ge(ln_ve[n], 3 * pair + 3)
                P.tensor_tensor(rstd[n][:, :], vrb[:, :], rt[:, :], ALU.mult).then_inc(ln_rs[n], 1)

            def combine(pair):
                gp.wait_ge(ve_s["wn"], pair + 1)
                P.tensor_tensor(wr[:, :], wn[:, :], mhalf[0:TP, :], ALU.pow).then_inc(po["wr"], 1)
                gp.wait_ge(po["wr"], pair + 1)
                gp.nop(nofuse=True)
                P.tensor_scalar(cs_scale[:, :], wr[:, :], cscale[0:TP, 0:1], 1.0, ALU.mult,
                                ALU.mult).then_inc(po["scale"], 1)
                root(0, pair)

            def pv(pair):
                root(1, pair)
                gp.wait_ge(ln_xn[1], G * pair + G)
                P.tensor_tensor(hx[:, :, :], res[1][:, :, :], xn[1][:, :, :], ALU.add).then_inc(po["hx"], 1)

            def ffn_down(pair):
                root(2, pair)
                root(3, pair)

            def usum(pair):
                for h in range(G):
                    gp.wait_ge(ac["us"], G * pair + h + 1)
                    gp.nop(nofuse=True)
                    P.tensor_scalar(ub[:, h, :], us[:, h, :], DECAY * 1e12, 1.0, ALU.mult,
                                    ALU.min).then_inc(po["ub"], 1)
                gp.wait_ge(ve_s["rt"], pair + 1)
                gp.wait_ge(ln_xn[3], G * pair + G)
                P.tensor_tensor(lnvr[:, :, :], xn[3][:, :, :], rt[:, :].unsqueeze(2).to_broadcast([TP, Q, D]),
                                ALU.mult).then_inc(po["lnvr"], 1)

            def linear(pair):
                scaled_root(4, pair)

            def embed(pair):
                scaled_root(5, pair)
                root(6, pair)
                root(7, pair)

            front = [combine, pv, ffn_down, usum, linear, embed]
            gp.wait_ge(cst_set, 1)
            gp.wait_ge(pack_in[0], 16)
            for stage in front:
                stage(0)
            with gp.Fori(1, NP) as pair:
                for stage in front:
                    stage(pair)


def kernel(**inputs):
    import numpy as _np
    import concourse.bacc as _bacc
    from concourse import mybir as _mybir
    from concourse.bass_utils import run_bass_kernel_spmd as _run

    a = {k: _np.asarray(v) for k, v in inputs.items()}
    f = _np.float32
    x = a["x"]
    x_T = _np.zeros((CIN, B, XC), f)
    x_T[:, :, 0:L] = x.transpose(2, 0, 1)
    x_nat = _np.ascontiguousarray(x.reshape(B, XP, XJ, CIN).transpose(1, 0, 2, 3))

    def rows(v, n=128):
        return _np.broadcast_to(v.reshape(1, -1), (n, v.size))

    def halves(w):
        return w.reshape(HC, 128, -1).transpose(1, 0, 2).reshape(128, -1)

    t = _np.arange(TT)
    band = _np.zeros((XP, XJ, TT), f)
    for j in range(XJ):
        d = XJ * _np.arange(XP)[:, None] + j - t[None, :]
        band[:, j] = (d >= 0) & (d < KW)
    smask = _np.concatenate([_np.where(t[None, :SW[i]] < (TP * i + _np.arange(TP))[:, None], 0.0, NEG)
                             for i in range(NT)], axis=1)
    rankc = _np.stack([_np.where(t[None, :T] < (TP * i + _np.arange(TP))[:, None], 0.0, TINY)
                       for i in range(NT)], axis=1)
    decay = []
    for i in range(NT):
        d = t[None, TP * i:] - (TP * i + _np.arange(TP))[:, None] - 1
        decay.append(_np.where(d >= 0, DECAY ** _np.maximum(d, 0).astype(_np.float64), 0.0))
    e = _np.arange(EXP)
    topc = _np.where(e[None, :] < e[:, None], 0.0, TINY)

    values = {
        "conv": a["L0_tok_kernel"].transpose(1, 0, 2).reshape(CIN, KW * D),
        "eye2": _np.concatenate([_np.eye(D), _np.eye(D)]), "band": band.reshape(XP, -1),
        "cbias": rows(a["L0_tok_bias"]), "cscale": rows(a["L0_tok_scale"]),
        "ident": _np.eye(128), "wq": a["L0_attn_Wq"], "wk": a["L0_attn_Wk"], "wvT": a["L0_attn_Wv"].T,
        "smask": smask, "wrB": _np.broadcast_to(a["L0_ffn_wr"], (D, TP)), "brB": rows(a["L0_ffn_br"]),
        "rankc": rankc.reshape(TP, -1), "fw1": a["L0_ffn_w1"], "fb1": a["L0_ffn_b1"].reshape(HC, 128).T,
        "fw2": halves(a["L0_ffn_w2"]), "fb2": rows(a["L0_ffn_b2"]),
        "dxT": a["L1_attn_Dx"].T, "ones": _np.ones((128, 128)), "decay": _np.concatenate(decay, axis=1),
        "dyT": a["L1_attn_Dy"].T, "eT": halves(a["L1_attn_E"].T), "rw": a["L1_ffn_Wr"],
        "rb": rows(a["L1_ffn_br"]), "topc": rows(topc), "eb2": a["L1_ffn_b2"],
        "w1": a["L1_ffn_W1"].transpose(1, 0, 2).reshape(D, -1), "gT": a["L1_ffn_ln_g"].T,
        "bT": a["L1_ffn_ln_b"].T, "b1": a["L1_ffn_b1"].reshape(EXP * HC, 128).T,
        "w2": a["L1_ffn_W2"].reshape(EXP * HC, 128, D).transpose(1, 0, 2).reshape(128, -1),
    }
    at, widths = fields()
    packs = [_np.zeros((128, w), f) for w in widths]
    for name, v in values.items():
        n, c, cols, nrows = at[name]
        packs[n][0:nrows, c:c + v.shape[1]] = v

    nc = _bacc.Bacc("TRN2", target_bir_lowering=False, num_devices=1)
    arrays = {"in_x_nat": x_nat, "in_x_T": x_T} | {f"in_pack{n}": p for n, p in enumerate(packs)}
    aps = {n: nc.dram_tensor(n, v.shape, _mybir.dt.from_np(v.dtype), kind="ExternalInput").ap()
           for n, v in arrays.items()}
    out = nc.dram_tensor("out_0_dram", (TP, B * NT, D), _mybir.dt.float32, kind="ExternalOutput").ap()
    build(nc, aps["in_x_nat"], aps["in_x_T"], [aps[f"in_pack{n}"] for n in range(len(packs))], out)
    r = _run(nc, [arrays], core_ids=[0])
    got = r.results[0]["out_0_dram"]
    return _np.ascontiguousarray(
        got.reshape(TP, B, NT, D).transpose(1, 2, 0, 3).reshape(B, TT, D)[:, :T])
```

```python
import numpy as np

import concourse.bass as bass
from concourse import mybir
from contextlib import ExitStack

B, L, CIN, KW, D = 8, 375, 128, 15, 64
T = L - KW + 1
TP, NT = 121, 3
TT = TP * NT
XC = 2 * (KW // 2) + TT + 1
XP, XJ = 125, 3
G = 2
NP = B // G
Q = G * NT
H = 256
HC = H // 128
EXP, TOPK = 8, 2
KEEP = max(1, T // 2) - 1
DECAY = 0.97
TAPS = (KW + 1) // 2
UNITS = EXP * G
TW = TT + 1
NEG = -1.0e10
TINY = float(np.finfo(np.float32).tiny)
SW = [T, 2 * TP, T]


def fields():
    groups = [
        [("conv", 2 * TAPS * D, CIN), ("eye2", D, 128), ("band", XJ * TT, XP), ("cbias", D, 128),
         ("cscale", 1, 128)],
        [("ident", 128, 128), ("wq", D, D), ("wk", D, D), ("wvT", D, D), ("smask", sum(SW), TP),
         ("wrB", TP, D), ("brB", 1, 128)],
        [("rankc", NT * T, TP), ("fw1", H, D), ("fb1", HC, 128), ("fw2", HC * D, 128), ("fb2", D, 128),
         ("dxT", H, D), ("ones", 128, 128), ("decay", 2 * TT, TP), ("dyT", H, D), ("eT", HC * D, 128),
         ("rw", EXP, 128), ("rb", EXP, 128), ("topc", EXP * EXP, 128), ("pick", G * G, 128),
         ("spread", EXP * 128, 2 * G * EXP)],
        [("w1", EXP * H, 128), ("gT", EXP, 128), ("bT", EXP, D), ("b1", EXP * HC, 128), ("eb2", EXP, 128),
         ("w2", EXP * HC * D, 128)],
    ]
    at = {}
    for n, group in enumerate(groups):
        c = 0
        for name, cols, rows in group:
            at[name] = (n, c, cols, rows)
            c += cols
    return at, [sum(g[1] for g in group) for group in groups]


def build(nc, x_nat, x_T, packs, out):
    f32 = mybir.dt.float32
    f32r = mybir.dt.float32r
    ALU = mybir.AluOpType
    ACT = mybir.ActivationFunctionType
    AX = mybir.AxisListType
    at, widths = fields()

    ctx = ExitStack()
    with ctx:
        def sb(name, shape, dt=f32):
            return ctx.enter_context(nc.sbuf_tensor(name, shape, dt))

        def sem(name):
            return ctx.enter_context(nc.semaphore(name))

        pack_sb = [sb(f"pack{n}", [128, w]) for n, w in enumerate(widths)]

        def field(name):
            n, c, cols, rows = at[name]
            return pack_sb[n][0:rows, c:c + cols]

        conv_w, eye2, cbias, cscale = field("conv"), field("eye2"), field("cbias"), field("cscale")
        band = field("band").rearrange("p (j t) -> p j t", j=XJ)
        ident, wq, wk, wvT, smask = (field(n) for n in ("ident", "wq", "wk", "wvT", "smask"))
        wrB, brB = field("wrB"), field("brB")
        rankc = field("rankc").rearrange("p (i t) -> p i t", i=NT)
        fw1, fb1, fb2 = field("fw1"), field("fb1"), field("fb2")
        fw2 = field("fw2").rearrange("p (c f) -> p c f", c=HC)
        dxT, dyT, ones, decay = field("dxT"), field("dyT"), field("ones"), field("decay")
        eT = field("eT").rearrange("p (c f) -> p c f", c=HC)
        rw, rb, eb2 = field("rw"), field("rb"), field("eb2")
        pick = field("pick").rearrange("p (h m) -> p h m", h=G)
        topc = field("topc").rearrange("p (e f) -> p e f", e=EXP)
        w1 = field("w1").rearrange("p (e n) -> p e n", e=EXP)
        gT, bT, b1 = field("gT"), field("bT"), field("b1")
        w2 = field("w2").rearrange("p (u f) -> p u f", f=D)

        wqk = sb("wqk", [D, D])
        w1s = sb("w1s", [128, 2, EXP, H], f32r)
        spread = sb("spread", [2 * G * EXP, EXP, 128], f32r)
        b1f = sb("b1f", [128, EXP * HC])
        mhalf = sb("mhalf", [128, Q])

        xnat = sb("xnat", [XP, G, XJ, CIN])
        sq = sb("sq", [XP, G * XJ])
        wn = sb("wn", [TP, Q])
        wr = sb("wr", [TP, Q])
        cs_scale = sb("cs_scale", [TP, Q])
        res = [sb(f"res{n}", [TP, Q, D]) for n in range(4)]
        LN = (0, 1, 2, 4, 5, 6)
        xn = {n: sb(f"xn{n}", [TP, Q, D]) for n in LN if n != 6}
        stats = {n: sb(f"stats{n}", [TP, Q, 6]) for n in LN}
        mv = {n: sb(f"mv{n}", [TP, Q, 2]) for n in LN}
        ve = {n: sb(f"ve{n}", [TP, Q]) for n in LN}
        rstd = {n: sb(f"rstd{n}", [TP, Q]) for n in LN}
        xc = {n: sb(f"xc{n}", [TP, Q, D]) for n in LN}
        probs = sb("probs", [TP, Q, TT])
        smax = sb("smax", [TP, Q])
        nmax = sb("nmax", [TP, Q])
        ssum = sb("ssum", [TP, Q])
        rsum = sb("rsum", [TP, Q])
        vv = sb("vv", [TP, Q, D])
        wB = sb("wB", [TP, G, T])
        ranks = probs
        crow = sb("crow", [TP, Q])
        cdiag = sb("cdiag", [TP, Q, TP])
        twice = sb("twice", [TP, Q])
        again = sb("again", [TP, Q])
        unagain = sb("unagain", [TP, Q])
        lnsc = sb("lnsc", [TP, Q])
        wcol = sb("wcol", [TP, Q])
        rank = sb("rank", [TP, Q])
        mw = sb("mw", [TP, Q])
        hx = sb("hx", [TP, Q, D])
        fy = sb("fy", [TP, Q, D])
        rt = sb("rt", [TP, Q])
        rsq = sb("rsq", [TP, Q])
        vra = sb("vra", [TP, Q])
        vrb = sb("vrb", [TP, Q])
        lnvr = sb("lnvr", [TP, Q, D])
        gd = sb("gd", [TP, G, 2 * TT])
        lg = sb("lg", [TP, Q, EXP])
        lmax = sb("lmax", [TP, Q])
        ex = sb("ex", [TP, Q, EXP])
        dif = sb("dif", [TP, Q, EXP, EXP])
        erank = sb("erank", [TP, Q, EXP])
        esel = sb("esel", [TP, Q, EXP])
        eden = sb("eden", [TP, Q])
        xT = sb("xT", [CIN, G, XC])
        cs = sb("cs", [128, G, TT])
        xnT = sb("xnT", [D, G, TT])
        gq = sb("gq", [D, G, TT])
        x2T = sb("x2T", [D, G, TT])
        hT = sb("hT", [128, G, HC, TT])
        vT = sb("vT", [D, G, TT])
        u = sb("u", [128, G, HC, TT])
        us = sb("us", [G, TT])
        ub = sb("ub", [G, TT])
        seen = sb("seen", [G, TT + 4])
        grow = sb("grow", [G, TT])
        fed = sb("fed", [G, TT])
        grown = sb("grown", [G, TT + 1])
        den = sb("den", [G, TT])
        den2 = sb("den2", [G, TT])
        z = sb("z", [128, G, HC, TT])
        naT = sb("naT", [D, G, TT])
        yT = hT
        x5 = sb("x5", [TP, Q, D])
        x5s = sb("x5s", [TP, Q, 2, D], f32r)
        x5T = sb("x5T", [128, G, TW], f32r)
        gate = sb("gate", [TP, NT, G, EXP])
        gates = sb("gates", [TP, NT, 2, G, EXP], f32r)
        gsT = sb("gsT", [2 * G * EXP, TW], f32r)
        gateB = sb("gateB", [128, EXP, TT])
        w1g = gateB[:, :, 0:H]
        hid = sb("hid", [128, 2, HC, TT])
        prod = sb("prod", [128, 2, TT])
        acc = sb("acc", [128, 2, TT])
        outb = sb("outb", [TP, Q, D])

        FA = [ctx.enter_context(nc.psum_tensor(f"FA{h}", [128, 512], f32)) for h in range(G)]
        FB = [ctx.enter_context(nc.psum_tensor(f"FB{h}", [128, 512], f32)) for h in range(G)]
        HB = [ctx.enter_context(nc.psum_tensor(f"HB{h}", [128, 512], f32)) for h in range(HC)]
        YB = [ctx.enter_context(nc.psum_tensor(f"YB{h}", [128, 512], f32)) for h in range(2)]

        x_in, pack_in, out_st = sem("x_in"), [sem(f"pack_in{n}") for n in range(len(widths))], sem("out_st")
        out_free = sem("out_free")
        cst_set, wqk_mm, wqk_set, w1g_set, w1hi_set, w1s_set, spread_set, b1f_mm, b1f_set = (sem(n) for n in (
            "cst_set", "wqk_mm", "wqk_set", "w1g_set", "w1hi_set", "w1s_set", "spread_set", "b1f_mm", "b1f_set"))
        pe = {n: sem("pe_" + n) for n in (
            "conv", "comb", "win", "t1", "proj", "sA", "v", "s2", "pv", "t2", "rt", "f1", "f2", "t3", "dx",
            "usum", "denT", "carry", "gram", "a", "t4", "dy", "e", "t5", "lg", "gT", "gB", "w1", "y", "out")}
        ac = {n: sem("act_" + n) for n in (
            "sq", "cslo", "xnT", "gq", "exp", "x2T", "hT", "vT", "u", "us", "naT", "x5T", "x5hi", "ex", "gsT",
            "gB", "hid")}
        ve_s = {n: sem("dve_" + n) for n in (
            "cshi", "wn", "res0", "scA", "sc2", "nmax", "rsum", "vv", "res1", "wB", "wcol", "rank", "mw", "fy",
            "fm", "res2", "var3", "var7", "seen", "ub", "grow", "fed", "grown", "den", "guard", "crow", "cdiag",
            "z", "rt", "rsq", "gd", "yT", "res3", "x5", "x5lo", "lg", "lb", "lmax", "lsub", "dif", "cmp",
            "erank", "esel", "eden", "erec", "gate", "ghi", "glo", "prod", "out")}
        po = {n: sem("pool_" + n) for n in (
            "wr", "scale", "hx", "again3", "again7", "unagain", "z0", "lnsc", "lnvr", "acc")}
        ln_st = sem("ln_st")
        ln_mv = {n: sem(f"ln_mv{n}") for n in LN}
        ln_ve = {n: sem(f"ln_ve{n}") for n in LN}
        ln_rs = {n: sem(f"ln_rs{n}") for n in LN}
        ln_xc = sem("ln_xc")
        ln_xn = {n: sem(f"ln_xn{n}") for n in LN}
        LN_EPS = 1e-5

        FINISH = 18

        block = ctx.enter_context(nc.Block())

        def tile_q(h, i):
            return NT * h + i

        @block.sync
        def _(sp):
            def load_x(pair, later=True):
                if later:
                    sp.wait_ge(pe["conv"], G * pair)
                    sp.wait_ge(ac["sq"], pair)
                sp.dma_start(xT[:, :, :], x_T[:, bass.ds(pair * G, G), :]).then_inc(x_in, 16)
                sp.dma_start(xnat[:, :, :, :], x_nat[:, bass.ds(pair * G, G), :, :]).then_inc(x_in, 16)

            def store(pair):
                sp.wait_ge(ve_s["out"], pair + 1)
                sp.dma_start(out[:, bass.ds(pair * Q, Q), :], outb[:, :, :]).then_inc(out_st, 16)
                sp.wait_ge(out_st, 16 * pair + 16)
                sp.sem_inc(out_free, 1)

            sp.dma_start(pack_sb[0][:, :], packs[0]).then_inc(pack_in[0], 16)
            sp.sem_inc(out_free, 1)
            load_x(0, later=False)
            for n in range(1, len(widths)):
                sp.dma_start(pack_sb[n][:, :], packs[n]).then_inc(pack_in[n], 16)
            load_x(1)
            with sp.Fori(0, NP - 2) as pair:
                load_x(pair + 2)
                store(pair)
            store(NP - 2)
            store(NP - 1)

        @block.tensor
        def _(te):
            mm = nc.tensor.matmul

            def tok(i):
                return slice(TP * i, TP * (i + 1))

            def transposes(dst, src, h, done):
                te.nop(nofuse=True)
                for i in range(NT):
                    last = nc.tensor.transpose(dst[0:D, tok(i)], src[:, tile_q(h, i), :], ident[0:TP, 0:TP])
                last.then_inc(done, 1)

            def to_hidden(w, src, h, c, dst):
                return mm(dst[:, 0:TT], w[:, 128 * c:128 * (c + 1)], src[:, h, :], start=True, stop=True)

            def from_hidden(src, w, dst):
                for i in range(NT):
                    for c in range(HC):
                        last = mm(dst[0:TP, D * i:D * (i + 1)], src[:, c, tok(i)], w[:, c, :],
                                  start=(c == 0), stop=(c == HC - 1))
                return last

            def conv(pair):
                te.wait_ge(x_in, 32 * (pair + 1))
                if not (isinstance(pair, int) and pair == 0):
                    te.wait_ge(ac["gB"], EXP * pair)
                for h in range(G):
                    for k in range(TAPS):
                        last = mm(FB[h][:, 0:TT + 1], conv_w[:, 2 * D * k:2 * D * (k + 1)],
                                  xT[:, h, 2 * k:2 * k + TT + 1], start=(k == 0), stop=(k == TAPS - 1))
                    last.then_inc(pe["conv"], 1)
                    if h == 0:
                        te.wait_ge(ac["sq"], pair + 1)
                        for i in range(NT):
                            for j in range(XJ):
                                last = mm(FA[1][0:TP, G * i:G * (i + 1)], band[:, j, tok(i)], sq[:, j::XJ],
                                          start=(j == 0), stop=(j == XJ - 1))
                        last.then_inc(pe["win"], 1)

            def combine(pair):
                for h in range(G):
                    te.wait_ge(ac["cslo"], G * pair + h + 1)
                    te.wait_ge(ve_s["cshi"], G * pair + h + 1)
                    if h == 1:
                        te.wait_ge(ve_s["wn"], pair + 1)
                    for i in range(NT):
                        last = mm(FA[h][0:TP, D * i:D * (i + 1)], cs[:, h, tok(i)], eye2, start=True, stop=True)
                    last.then_inc(pe["comb"], 1)
            def t1(pair):
                for h in range(G):
                    te.wait_ge(ln_xn[0], G * pair + h + 1)
                    transposes(FA[h], xn[0], h, pe["t1"])

            def proj(pair):
                for h in range(G):
                    te.wait_ge(ac["xnT"], G * pair + h + 1)
                    te.nop(nofuse=True)
                    mm(FB[h][0:D, 0:TT], wqk[:, :], xnT[:, h, :], start=True, stop=True).then_inc(pe["proj"], 1)

            def scores_a(pair):
                for h in range(G):
                    te.wait_ge(ac["gq"], G * pair + h + 1)
                    for n, bank in enumerate((FA[h], FB[h])):
                        mm(bank[0:TP, 0:SW[n]], xnT[:, h, tok(n)], gq[:, h, 0:SW[n]],
                           start=True, stop=True).then_inc(pe["sA"], 1)

            def scores_b(pair):
                for h in range(G):
                    te.wait_ge(ve_s["scA"], 2 * (G * pair + h) + 2)
                    mm(FB[h][0:TP, 0:SW[2]], xnT[:, h, tok(2)], gq[:, h, 0:SW[2]],
                       start=True, stop=True).then_inc(pe["s2"], 1)
                    for i in range(NT):
                        last = mm(FA[h][0:TP, D * i:D * (i + 1)], xnT[:, h, tok(i)], wvT, start=True, stop=True)
                    last.then_inc(pe["v"], 1)

            def pv(pair):
                for h in range(G):
                    te.wait_ge(ve_s["vv"], G * pair + h + 1)
                    for i in range(NT):
                        keys = [0, 1, 2] if i < 2 else [0, 2]
                        for k in keys:
                            rows = min(TP, T - TP * k)
                            last = mm(FB[h][0:TP, D * i:D * (i + 1)], probs[0:rows, tile_q(h, k), tok(i)],
                                      vv[0:rows, tile_q(h, k), :], start=(k == 0), stop=(k == keys[-1]))
                    last.then_inc(pe["pv"], 1)

            def t2(pair):
                for h in range(G):
                    te.wait_ge(ln_xn[1], G * pair + h + 1)
                    transposes(FA[h], xn[1], h, pe["t2"])

            def router(pair):
                for h in range(G):
                    te.wait_ge(ac["x2T"], G * pair + h + 1)
                    mm(FB[h][0:TP, 0:T], wrB, x2T[:, h, 0:T], start=True, stop=True).then_inc(pe["rt"], 1)

            def ffn_up(pair):
                for h in range(G):
                    to_hidden(fw1, x2T, h, 0, FA[h]).then_inc(pe["f1"], 1)
                for h in range(G):
                    te.wait_ge(ve_s["wB"], G * pair + h + 1)
                    to_hidden(fw1, x2T, h, 1, FB[h]).then_inc(pe["f1"], 1)

            def ffn_down(pair):
                for h in range(G):
                    te.wait_ge(ac["hT"], HC * G * pair + G + h + 1)
                    from_hidden(hT[:, h, :, :], fw2, FA[h]).then_inc(pe["f2"], 1)

            def t3(pair):
                for h in range(G):
                    te.wait_ge(ln_xn[2], G * pair + h + 1)
                    transposes(FB[h], xn[2], h, pe["t3"])

            def dx(pair):
                for h in range(G):
                    te.wait_ge(ac["vT"], G * pair + h + 1)
                    to_hidden(dxT, vT, h, 0, FA[h]).then_inc(pe["dx"], 1)
                for h in range(G):
                    to_hidden(dxT, vT, h, 1, FB[h]).then_inc(pe["dx"], 1)

            def usum(pair):
                te.wait_ge(ac["u"], HC * G * pair + HC * G)
                for n in range(HC * G):
                    last = mm(FA[0][0:G, 0:TT], pick[:, n // HC, :], u[:, n // HC, n % HC, :],
                              start=(n == 0), stop=(n == HC * G - 1))
                last.then_inc(pe["usum"], 1)

            def denoms(pair):
                te.wait_ge(ve_s["guard"], pair + 1)
                te.nop(nofuse=True)
                for i in range(NT):
                    last = nc.tensor.transpose(FB[0][0:TP, G * i:G * (i + 1)], den2[:, tok(i)], ident[0:G, 0:G])
                last.then_inc(pe["denT"], 1)
                te.wait_ge(ve_s["cdiag"], pair + 1)
                for h in range(G):
                    mm(FA[h][:, 0:TT], ones[0:TP, :], cdiag[:, NT * h:NT * (h + 1), :],
                       start=True, stop=True).then_inc(pe["carry"], 1)

            def gram(pair):
                for h in range(G):
                    te.wait_ge(ve_s["z"], G * pair + h + 1)
                    if h == 0:
                        te.wait_ge(po["z0"], pair + 1)
                    for bank, tiles in ((FA[h], (0,)), (FB[h], (1, 2))):
                        at_col = 0
                        for i in tiles:
                            w = TT - TP * i
                            for c in range(HC):
                                last = mm(bank[0:TP, at_col:at_col + w], z[:, h, c, tok(i)],
                                          z[:, h, c, TP * i:TT], start=(c == 0), stop=(c == HC - 1))
                            at_col += w
                        last.then_inc(pe["gram"], 1)

            def linear(pair):
                te.wait_ge(po["lnvr"], 2 * pair + 2)
                for h in range(G):
                    te.wait_ge(ve_s["gd"], 2 * (G * pair + h) + 2)
                    for k in range(NT):
                        for i in range(k + 1):
                            first = (0, TT, TT + 2 * TP)[i] + TP * (k - i)
                            last = mm(FA[h][0:TP, D * k:D * (k + 1)], gd[:, h, first:first + TP],
                                      lnvr[:, tile_q(h, i), :], start=(i == 0), stop=(i == k))
                    last.then_inc(pe["a"], 1)

            def t4(pair):
                for h in range(G):
                    te.wait_ge(ln_xn[4], G * pair + h + 1)
                    transposes(FB[h], xn[4], h, pe["t4"])

            def dy(pair):
                for h in range(G):
                    te.wait_ge(ac["naT"], G * pair + h + 1)
                    to_hidden(dyT, naT, h, 0, FA[h]).then_inc(pe["dy"], 1)
                for h in range(G):
                    to_hidden(dyT, naT, h, 1, FB[h]).then_inc(pe["dy"], 1)

            def embed(pair):
                for h in range(G):
                    te.wait_ge(ve_s["yT"], HC * G * pair + G + h + 1)
                    from_hidden(yT[:, h, :, :], eT, FA[h]).then_inc(pe["e"], 1)

            def t5(pair):
                te.wait_ge(ac["x5hi"], pair + 1)
                te.wait_ge(ve_s["x5lo"], pair + 1)
                for h in range(G):
                    te.nop(nofuse=True)
                    for i in range(NT):
                        last = nc.tensor.transpose(
                            FB[h][:, tok(i)], x5s[:, tile_q(h, i), :, :].rearrange("p s f -> p (s f)").bitcast(f32),
                            ident[0:TP, 0:TP])
                    last.then_inc(pe["t5"], 1)

            def route(pair):
                for h in range(G):
                    te.wait_ge(ac["x5T"], G * pair + h + 1)
                    for i in range(NT):
                        last = mm(FA[h][0:TP, EXP * i:EXP * (i + 1)], x5T[:, h, tok(i)].bitcast(f32), rw,
                                  start=True, stop=True)
                    last.then_inc(pe["lg"], 1)
                te.wait_ge(ve_s["glo"], pair + 1)
                te.wait_ge(ve_s["ghi"], pair + 1)
                te.nop(nofuse=True)
                for i in range(NT):
                    last = nc.tensor.transpose(
                        FB[0][0:2 * G * EXP, tok(i)],
                        gates[:, i, :, :, :].rearrange("p s h e -> p (s h e)").bitcast(f32), ident[0:TP, 0:TP])
                last.then_inc(pe["gT"], 1)
                te.wait_ge(ac["gsT"], pair + 1)
                for e in range(EXP):
                    if e >= 4:
                        te.wait_ge(ac["gB"], EXP * pair + e - 3)
                    mm((FA + FB)[e % 4][:, 0:TW], spread[:, e, :], gsT[:, :],
                       start=True, stop=True).then_inc(pe["gB"], 1)

            def up(pair, n):
                e, h = n // G, n % G
                for c in range(HC):
                    if n:
                        te.wait_ge(ac["hid"], HC * (UNITS * pair + n - 1) + c + 1)
                    for part in range(2):
                        last = mm(HB[c][:, 0:TW], w1s[:, part, e, 128 * c:128 * (c + 1)], x5T[:, h, :],
                                  start=(part == 0), stop=(part == 1))
                    last.then_inc(pe["w1"], 1)

            def down(pair, n):
                e, h = n // G, n % G
                te.wait_ge(ac["hid"], HC * (UNITS * pair + n) + HC)
                if e >= 2 and h == 0:
                    te.wait_ge(ve_s["prod"], EXP * pair + e - 1)
                for c in range(HC):
                    last = mm(YB[e % 2][D * h:D * (h + 1), 0:TT], w2[:, HC * e + c, :], hid[:, n % 2, c, :],
                              start=(c == 0), stop=(c == HC - 1))
                last.then_inc(pe["y"], 1)

            def finish(pair):
                te.wait_ge(po["acc"], EXP * pair + EXP)
                te.nop(nofuse=True)
                for i in range(NT):
                    last = nc.tensor.transpose(YB[0][0:TP, 128 * i:128 * (i + 1)], acc[:, EXP % 2, tok(i)], ident)
                last.then_inc(pe["out"], 1)

            front = [conv, combine, t1, proj, scores_a, scores_b, pv, t2, router, ffn_up, ffn_down, t3, dx,
                     usum, denoms, gram, linear, t4, dy, embed, t5, route]

            def experts(pair, n):
                if n < UNITS:
                    up(pair, n)
                if 0 < n <= UNITS:
                    down(pair, n - 1)
                if n == FINISH:
                    finish(pair)

            te.wait_ge(pack_in[0], 16)
            conv(0)
            te.wait_ge(pack_in[1], 16)
            mm(HB[0][0:D, 0:D], wq, wk, start=True, stop=True).then_inc(wqk_mm, 1)
            combine(0)
            t1(0)
            te.wait_ge(wqk_set, 1)
            te.wait_ge(pack_in[2], 16)
            te.wait_ge(pack_in[3], 16)
            for n in range(EXP * HC):
                e, c = n // HC, n % HC
                last = mm(HB[1][:, n:n + 1], w1[0:D, e, 128 * c:128 * (c + 1)], bT[:, e:e + 1], start=True, stop=True)
            last.then_inc(b1f_mm, 1)
            for stage in front[3:21]:
                stage(0)
            te.wait_ge(spread_set, 1)
            route(0)
            te.wait_ge(w1s_set, 1)
            te.wait_ge(b1f_set, 1)
            with te.Fori(0, NP - 1) as pair:
                for n, stage in enumerate(front):
                    stage(pair + 1)
                    experts(pair, n)
            for n in range(FINISH + 1):
                experts(NP - 1, n)

        @block.scalar
        def _(se):
            act = nc.scalar.activation

            def from_bank(dst, bank, h, pair, produced, done):
                se.wait_ge(produced, G * pair + h + 1)
                act(dst[:, h, :], bank[h][0:D, 0:TT], ACT.Copy).then_inc(done, 1)

            def conv(pair):
                se.wait_ge(x_in, 32 * (pair + 1))
                for h in range(G):
                    for j in range(XJ):
                        last = act(xnat[:, h, j, :], xnat[:, h, j, :], ACT.Square,
                                   accum_out=sq[:, XJ * h + j:XJ * h + j + 1])
                last.then_inc(ac["sq"], 1)
                for h in range(G):
                    se.wait_ge(pe["conv"], G * pair + h + 1)
                    act(cs[0:D, h, :], FB[h][0:D, 0:TT], ACT.Copy).then_inc(ac["cslo"], 1)

            def t1(pair):
                for h in range(G):
                    from_bank(xnT, FA, h, pair, pe["t1"], ac["xnT"])

            def proj(pair):
                for h in range(G):
                    from_bank(gq, FB, h, pair, pe["proj"], ac["gq"])

            def scores_b(pair):
                se.wait_ge(ve_s["nmax"], pair + 1)
                for h in range(G):
                    for i in range(NT):
                        q = tile_q(h, i)
                        last = act(probs[:, q, 0:SW[i]], probs[:, q, 0:SW[i]], ACT.Exp, bias=nmax[:, q:q + 1],
                                   accum_out=ssum[:, q:q + 1])
                    last.then_inc(ac["exp"], 1)

            def t2(pair):
                for h in range(G):
                    from_bank(x2T, FA, h, pair, pe["t2"], ac["x2T"])

            def ffn_up(pair):
                for n in range(HC * G):
                    c, h = n // G, n % G
                    se.wait_ge(pe["f1"], HC * G * pair + n + 1)
                    act(hT[:, h, c, :], (FA, FB)[c][h][:, 0:TT], ACT.Gelu_apprx_tanh,
                        bias=fb1[:, c:c + 1]).then_inc(ac["hT"], 1)

            def t3(pair):
                for h in range(G):
                    from_bank(vT, FB, h, pair, pe["t3"], ac["vT"])

            def dx(pair):
                for n in range(HC * G):
                    c, h = n // G, n % G
                    se.wait_ge(pe["dx"], HC * G * pair + n + 1)
                    act(u[:, h, c, :], (FA, FB)[c][h][:, 0:TT], ACT.Relu).then_inc(ac["u"], 1)

            def usum(pair):
                se.wait_ge(pe["usum"], pair + 1)
                act(us[:, :], FA[0][0:G, 0:TT], ACT.Copy, scale=1.0 / DECAY).then_inc(ac["us"], 1)

            def t4(pair):
                for h in range(G):
                    from_bank(naT, FB, h, pair, pe["t4"], ac["naT"])

            def t5(pair):
                se.wait_ge(ve_s["x5"], pair + 1)
                act(x5s[:, :, 0, :], x5[:, :, :], ACT.Copy).then_inc(ac["x5hi"], 1)
                for h in range(G):
                    se.wait_ge(pe["t5"], G * pair + h + 1)
                    act(x5T[:, h, 0:TT], FB[h][:, 0:TT], ACT.Copy).then_inc(ac["x5T"], 1)

            def route(pair):
                se.wait_ge(ve_s["lsub"], pair + 1)
                act(ex[:, :, :], lg[:, :, :], ACT.Exp).then_inc(ac["ex"], 1)
                se.wait_ge(pe["gT"], pair + 1)
                act(gsT[:, 0:TT], FB[0][0:2 * G * EXP, 0:TT], ACT.Copy).then_inc(ac["gsT"], 1)
                for e in range(EXP):
                    se.wait_ge(pe["gB"], EXP * pair + e + 1)
                    act(gateB[:, e, :], (FA + FB)[e % 4][:, 0:TT], ACT.Copy).then_inc(ac["gB"], 1)

            def experts(pair, n):
                if n >= UNITS:
                    return
                e = n // G
                if n >= 2:
                    se.wait_ge(pe["y"], UNITS * pair + n - 1)
                for c in range(HC):
                    se.wait_ge(pe["w1"], HC * (UNITS * pair + n) + c + 1)
                    act(hid[:, n % 2, c, :], HB[c][:, 0:TT], ACT.Gelu,
                        bias=b1f[:, HC * e + c:HC * e + c + 1]).then_inc(ac["hid"], 1)

            def none(pair):
                pass

            front = [conv, none, t1, proj, none, scores_b, none, t2, none, ffn_up, none, t3, dx,
                     usum, none, none, none, t4, none, none, t5, route]
            conv(0)
            se.wait_ge(wqk_mm, 1)
            act(wqk[:, :], HB[0][0:D, 0:D], ACT.Copy).then_inc(wqk_set, 1)
            for stage in front[1:]:
                if stage is ffn_up:
                    se.wait_ge(pack_in[2], 16)
                    act(spread[:, :, :], field("spread").rearrange("p (e m) -> p e m", e=EXP),
                        ACT.Copy).then_inc(spread_set, 1)
                stage(0)
            se.wait_ge(b1f_set, 1)
            with se.Fori(0, NP - 1) as pair:
                for n, stage in enumerate(front):
                    stage(pair + 1)
                    experts(pair, n)
            for n in range(UNITS):
                experts(NP - 1, n)

        @block.vector
        def _(dv):
            V = nc.vector

            def each(ap):
                return ap.unsqueeze(2).to_broadcast([TP, ap.shape[1], D])

            def ln_stats(n, source, pair):
                for q in range(Q):
                    last = V.bn_stats(stats[n][:, q, :], source(q))
                last.then_inc(ln_st, 1)
                dv.wait_ge(ln_st, len(LN) * pair + LN.index(n) + 1)
                dv.nop(nofuse=True)
                for q in range(Q):
                    last = V.bn_aggr(mv[n][:, q, :], stats[n][:, q, :])
                last.then_inc(ln_mv[n], 1)

            def center(n, halves, pair):
                dv.wait_ge(ln_mv[n], pair + 1)
                w = Q // len(halves)
                for k, source in enumerate(halves):
                    last = V.tensor_tensor(xc[n][:, w * k:w * (k + 1), :], source,
                                           each(mv[n][:, w * k:w * (k + 1), 0]), ALU.subtract)
                last.then_inc(ln_xc, 1)
                dv.wait_ge(ln_xc, len(LN) * pair + LN.index(n) + 1)
                dv.wait_ge(ln_rs[n], pair + 1)

            def normalise(n, halves, pair):
                center(n, halves, pair)
                for h in range(G):
                    V.tensor_tensor(xn[n][:, NT * h:NT * (h + 1), :], xc[n][:, NT * h:NT * (h + 1), :],
                                    each(rstd[n][:, NT * h:NT * (h + 1)]), ALU.mult).then_inc(ln_xn[n], 1)

            def layernorm(n, src, pair):
                ln_stats(n, lambda q: src[:, q, :], pair)
                normalise(n, [src[:, :, :]], pair)

            def tiles(bank):
                return [bank[h][0:TP, 0:NT * D].rearrange("p (i f) -> p i f", i=NT) for h in range(G)]

            def in_bank(bank):
                return lambda q: bank[q // NT][0:TP, D * (q % NT):D * (q % NT + 1)]

            def conv(pair):
                for h in range(G):
                    dv.wait_ge(pe["conv"], G * pair + h + 1)
                    V.tensor_copy(cs[D:128, h, :], FB[h][D:128, 1:TT + 1]).then_inc(ve_s["cshi"], 1)

            def combine(pair):
                dv.wait_ge(pe["win"], pair + 1)
                V.tensor_scalar(wn[:, :].rearrange("p (h i) -> p i h", h=G),
                                FA[1][0:TP, 0:Q].rearrange("p (i h) -> p i h", h=G),
                                1e-7, None, ALU.add).then_inc(ve_s["wn"], 1)
                dv.wait_ge(po["scale"], pair + 1)
                dv.wait_ge(pe["comb"], G * pair + G)
                for q in range(Q):
                    last = V.scalar_tensor_tensor(res[0][:, q, :], in_bank(FA)(q), cs_scale[:, q:q + 1],
                                                  cbias[0:TP, :], ALU.mult, ALU.add)
                last.then_inc(ve_s["res0"], 1)
                dv.wait_ge(ve_s["res0"], pair + 1)
                layernorm(0, res[0], pair)

            def score_tile(h, n, bank, done):
                q = tile_q(h, n)
                V.tensor_tensor_reduce(out=probs[:, q, 0:SW[n]], in0=bank[0:TP, 0:SW[n]],
                                       in1=smask[:, sum(SW[:n]):sum(SW[:n + 1])], scale=D ** -0.5,
                                       scalar=-3.0e38, op0=ALU.add, op1=ALU.max,
                                       accum_out=smax[:, q:q + 1]).then_inc(done, 1)

            def scores_a(pair):
                for h in range(G):
                    for n, bank in enumerate((FA[h], FB[h])):
                        dv.wait_ge(pe["sA"], 2 * (G * pair + h) + n + 1)
                        dv.nop(nofuse=True)
                        score_tile(h, n, bank, ve_s["scA"])

            def scores_b(pair):
                for h in range(G):
                    dv.wait_ge(pe["s2"], G * pair + h + 1)
                    dv.nop(nofuse=True)
                    score_tile(h, 2, FB[h], ve_s["sc2"])
                dv.wait_ge(ve_s["sc2"], G * pair + G)
                V.tensor_scalar(nmax[:, :], smax[:, :], -1.0, None, ALU.mult).then_inc(ve_s["nmax"], 1)
                dv.wait_ge(ac["exp"], G * pair + G)
                V.reciprocal(rsum[:, :], ssum[:, :]).then_inc(ve_s["rsum"], 1)
                dv.wait_ge(ve_s["rsum"], pair + 1)
                for h in range(G):
                    dv.wait_ge(pe["v"], G * pair + h + 1)
                    V.tensor_tensor(vv[:, NT * h:NT * (h + 1), :],
                                    FA[h][0:TP, 0:NT * D].rearrange("p (i f) -> p i f", i=NT),
                                    each(rsum[:, NT * h:NT * (h + 1)]), ALU.mult).then_inc(ve_s["vv"], 1)

            def pv(pair):
                for h in range(G):
                    dv.wait_ge(pe["pv"], G * pair + h + 1)
                    V.tensor_tensor(res[1][:, NT * h:NT * (h + 1), :],
                                    FB[h][0:TP, 0:NT * D].rearrange("p (i f) -> p i f", i=NT),
                                    res[0][:, NT * h:NT * (h + 1), :], ALU.add).then_inc(ve_s["res1"], 1)
                dv.wait_ge(ve_s["res1"], G * pair + G)
                layernorm(1, res[1], pair)

            def diagonal(dst, row, h):
                for i in range(NT):
                    w = min(TP, T - TP * i)
                    last = V.tensor_tensor_reduce(out=ranks[:, tile_q(h, i), 0:w], in0=row[:, TP * i:TP * i + w],
                                                  in1=ident[0:TP, 0:w], scale=1.0, scalar=0.0, op0=ALU.mult,
                                                  op1=ALU.add, accum_out=dst[:, tile_q(h, i):tile_q(h, i) + 1])
                return last

            def router(pair):
                for h in range(G):
                    dv.wait_ge(pe["rt"], G * pair + h + 1)
                    V.tensor_scalar(wB[:, h, :], FB[h][0:TP, 0:T], brB[0:TP, 0:1], None,
                                    ALU.add).then_inc(ve_s["wB"], 1)
                dv.wait_ge(ve_s["wB"], G * pair + G)
                for h in range(G):
                    last = diagonal(wcol, wB[:, h, :], h)
                last.then_inc(ve_s["wcol"], 1)
                dv.wait_ge(ve_s["wcol"], pair + 1)
                for h in range(G):
                    for i in range(NT):
                        q = tile_q(h, i)
                        last = V.scalar_tensor_tensor(ranks[:, q, 0:T], wB[:, h, :], wcol[:, q:q + 1], rankc[:, i, :],
                                                      ALU.subtract, ALU.is_ge, accum_out=rank[:, q:q + 1])
                last.then_inc(ve_s["rank"], 1)
                dv.wait_ge(ve_s["rank"], pair + 1)
                V.scalar_tensor_tensor(mw[:, :], rank[:, :], float(KEEP), wcol[:, :], ALU.is_lt,
                                       ALU.mult).then_inc(ve_s["mw"], 1)

            def ffn_down(pair):
                for h in range(G):
                    dv.wait_ge(pe["f2"], G * pair + h + 1)
                    V.tensor_tensor(fy[:, NT * h:NT * (h + 1), :],
                                    FA[h][0:TP, 0:NT * D].rearrange("p (i f) -> p i f", i=NT),
                                    fb2[0:TP, :].unsqueeze(1).to_broadcast([TP, NT, D]),
                                    ALU.add).then_inc(ve_s["fy"], 1)
                dv.wait_ge(ve_s["fy"], G * pair + G)
                dv.wait_ge(ve_s["mw"], pair + 1)
                dv.wait_ge(po["hx"], pair + 1)
                V.tensor_tensor(fy[:, :, :], fy[:, :, :], each(mw[:, :]), ALU.mult).then_inc(ve_s["fm"], 1)
                dv.wait_ge(ve_s["fm"], pair + 1)
                V.tensor_tensor(res[2][:, :, :], fy[:, :, :], hx[:, :, :], ALU.add).then_inc(ve_s["res2"], 1)
                dv.wait_ge(ve_s["res2"], pair + 1)
                layernorm(2, res[2], pair)
                twice_var(2, "var3", pair)

            def twice_var(n, done, pair):
                V.tensor_tensor(twice[:, :], mv[n][:, :, 1], rstd[n][:, :], ALU.mult).then_inc(ve_s[done], 1)
                dv.wait_ge(ve_s[done], 2 * pair + 1)
                V.tensor_tensor(twice[:, :], twice[:, :], rstd[n][:, :], ALU.mult).then_inc(ve_s[done], 1)

            def usum(pair):
                dv.wait_ge(ac["us"], pair + 1)
                V.tensor_tensor_scan(seen[:, 4:TT + 4], us[:, :], us[:, :], 0.0, ALU.max,
                                     ALU.max).then_inc(ve_s["seen"], 1)
                V.tensor_scalar(ub[:, :], us[:, :], DECAY * 1e12, 1.0, ALU.mult, ALU.min).then_inc(ve_s["ub"], 1)
                dv.wait_ge(ve_s["seen"], pair + 1)
                V.tensor_scalar(grow[:, :], seen[:, 0:TT], 0.0, DECAY * 1e12, ALU.is_equal,
                                ALU.mult).then_inc(ve_s["grow"], 1)
                dv.wait_ge(ve_s["ub"], pair + 1)
                V.scalar_tensor_tensor(fed[:, :], seen[:, 1:TT + 1], 0.0, ub[:, :], ALU.is_gt,
                                       ALU.add).then_inc(ve_s["fed"], 1)
                dv.wait_ge(ve_s["fed"], pair + 1)
                V.tensor_tensor_scan(grown[:, 1:TT + 1], grow[:, :], fed[:, :], 0.0, ALU.mult,
                                     ALU.add).then_inc(ve_s["grown"], 1)
                dv.wait_ge(ve_s["grown"], pair + 1)
                V.scalar_tensor_tensor(den[:, :], grown[:, 0:TT], 1.0, us[:, :], ALU.min,
                                       ALU.add).then_inc(ve_s["den"], 1)
                dv.wait_ge(ve_s["den"], pair + 1)
                V.tensor_scalar(den2[:, :], den[:, :], 1e-12 / DECAY, None, ALU.max).then_inc(ve_s["guard"], 1)

            def denoms(pair):
                dv.wait_ge(pe["denT"], pair + 1)
                V.reciprocal(crow[:, :].rearrange("p (h i) -> p i h", h=G),
                             FB[0][0:TP, 0:Q].rearrange("p (i h) -> p i h", h=G)).then_inc(ve_s["crow"], 1)
                dv.wait_ge(ve_s["crow"], pair + 1)
                V.tensor_tensor(cdiag[:, :, :], ident[0:TP, 0:TP].unsqueeze(1).to_broadcast([TP, Q, TP]),
                                crow[:, :].unsqueeze(2).to_broadcast([TP, Q, TP]), ALU.mult).then_inc(ve_s["cdiag"], 1)
                V.tensor_scalar(rt[:, :], crow[:, :], 1.0 / DECAY, None, ALU.mult).then_inc(ve_s["rt"], 1)
                dv.wait_ge(ve_s["rt"], pair + 1)
                V.tensor_tensor(rsq[:, :], rt[:, :], rt[:, :], ALU.mult).then_inc(ve_s["rsq"], 1)
                for h in range(G):
                    dv.wait_ge(pe["carry"], G * pair + h + 1)
                    for c in range(HC):
                        last = V.tensor_tensor_scan(z[:, h, c, 1:TT], FA[h][:, 0:TT - 1], u[:, h, c, 1:TT],
                                                    u[:, h, c, 0:1], ALU.mult, ALU.add)
                    last.then_inc(ve_s["z"], 1)

            def gram(pair):
                for h in range(G):
                    for n, bank in enumerate((FA[h], FB[h])):
                        dv.wait_ge(pe["gram"], 2 * (G * pair + h) + n + 1)
                        V.tensor_tensor(gd[:, h, TT * n:TT * (n + 1)], bank[0:TP, 0:TT],
                                        decay[:, TT * n:TT * (n + 1)], ALU.mult).then_inc(ve_s["gd"], 1)

            def linear(pair):
                dv.wait_ge(pe["a"], G * pair + G)
                ln_stats(4, in_bank(FA), pair)
                normalise(4, tiles(FA), pair)

            def dy(pair):
                for n in range(HC * G):
                    c, h = n // G, n % G
                    dv.wait_ge(pe["dy"], HC * G * pair + n + 1)
                    V.scalar_tensor_tensor(yT[:, h, c, :], (FA, FB)[c][h][:, 0:TT], 0.0, z[:, h, c, :],
                                           ALU.max, ALU.mult).then_inc(ve_s["yT"], 1)

            def embed(pair):
                dv.wait_ge(pe["e"], G * pair + G)
                ln_stats(5, in_bank(FA), pair)
                normalise(5, tiles(FA), pair)
                dv.wait_ge(ln_xn[5], G * pair + G)
                V.tensor_tensor(res[3][:, :, :], xn[5][:, :, :], res[2][:, :, :], ALU.add).then_inc(ve_s["res3"], 1)
                dv.wait_ge(ve_s["res3"], pair + 1)
                ln_stats(6, lambda q: res[3][:, q, :], pair)
                center(6, [res[3][:, :, :]], pair)
                twice_var(6, "var7", pair)
                dv.wait_ge(po["lnsc"], pair + 1)
                V.tensor_tensor(x5[:, :, :], xc[6][:, :, :], each(lnsc[:, :]), ALU.mult).then_inc(ve_s["x5"], 1)
                dv.wait_ge(ac["x5hi"], pair + 1)
                V.tensor_tensor(x5s[:, :, 1, :], x5[:, :, :], x5s[:, :, 0, :].bitcast(f32),
                                ALU.subtract).then_inc(ve_s["x5lo"], 1)

            def per_expert(ap):
                return ap.unsqueeze(2).to_broadcast([TP, Q, EXP])

            def route(pair):
                dv.wait_ge(po["unagain"], pair + 1)
                for h in range(G):
                    dv.wait_ge(pe["lg"], G * pair + h + 1)
                    V.tensor_tensor(lg[:, NT * h:NT * (h + 1), :],
                                    FA[h][0:TP, 0:NT * EXP].rearrange("p (i e) -> p i e", i=NT),
                                    unagain[:, NT * h:NT * (h + 1)].unsqueeze(2).to_broadcast([TP, NT, EXP]),
                                    ALU.mult).then_inc(ve_s["lg"], 1)
                dv.wait_ge(ve_s["lg"], G * pair + G)
                V.tensor_tensor(lg[:, :, :], lg[:, :, :], rb[0:TP, :].unsqueeze(1).to_broadcast([TP, Q, EXP]),
                                ALU.add).then_inc(ve_s["lb"], 1)
                dv.wait_ge(ve_s["lb"], pair + 1)
                V.reduce_max(lmax[:, :], lg[:, :, :], AX.X).then_inc(ve_s["lmax"], 1)
                dv.wait_ge(ve_s["lmax"], pair + 1)
                V.tensor_tensor(lg[:, :, :], lg[:, :, :], per_expert(lmax[:, :]),
                                ALU.subtract).then_inc(ve_s["lsub"], 1)
                dv.wait_ge(ac["ex"], pair + 1)
                V.tensor_tensor(dif[:, :, :, :], ex[:, :, :].unsqueeze(2).to_broadcast([TP, Q, EXP, EXP]),
                                ex[:, :, :].unsqueeze(3).to_broadcast([TP, Q, EXP, EXP]),
                                ALU.subtract).then_inc(ve_s["dif"], 1)
                dv.wait_ge(ve_s["dif"], pair + 1)
                V.tensor_tensor(dif[:, :, :, :], dif[:, :, :, :],
                                topc[0:TP, :, :].unsqueeze(1).to_broadcast([TP, Q, EXP, EXP]),
                                ALU.is_ge).then_inc(ve_s["cmp"], 1)
                dv.wait_ge(ve_s["cmp"], pair + 1)
                V.reduce_sum(erank[:, :, :], dif[:, :, :, :], AX.X).then_inc(ve_s["erank"], 1)
                dv.wait_ge(ve_s["erank"], pair + 1)
                V.scalar_tensor_tensor(esel[:, :, :], erank[:, :, :], float(TOPK), ex[:, :, :], ALU.is_lt,
                                       ALU.mult).then_inc(ve_s["esel"], 1)
                dv.wait_ge(ve_s["esel"], pair + 1)
                V.reduce_sum(eden[:, :], esel[:, :, :], AX.X).then_inc(ve_s["eden"], 1)
                dv.wait_ge(ve_s["eden"], pair + 1)
                V.reciprocal(eden[:, :], eden[:, :]).then_inc(ve_s["erec"], 1)
                dv.wait_ge(ve_s["erec"], pair + 1)
                V.tensor_tensor(gate[:, :, :, :].rearrange("p i h e -> p h i e"),
                                esel[:, :, :].rearrange("p (h i) e -> p h i e", h=G),
                                eden[:, :].rearrange("p (h i) -> p h i", h=G).unsqueeze(3).to_broadcast(
                                    [TP, G, NT, EXP]), ALU.mult).then_inc(ve_s["gate"], 1)
                dv.wait_ge(ve_s["gate"], pair + 1)
                V.tensor_copy(gates[:, :, 0, :, :], gate[:, :, :, :]).then_inc(ve_s["ghi"], 1)
                dv.wait_ge(ve_s["ghi"], pair + 1)
                V.tensor_tensor(gates[:, :, 1, :, :], gate[:, :, :, :], gates[:, :, 0, :, :].bitcast(f32),
                                ALU.subtract).then_inc(ve_s["glo"], 1)

            def experts(pair, n):
                e = n // G - 1
                if n % G == 0 and 0 <= e < EXP:
                    dv.wait_ge(pe["y"], UNITS * pair + G * (e + 1))
                    if e == 0:
                        dv.wait_ge(ac["gB"], EXP * pair + EXP)
                    if e >= 2:
                        dv.wait_ge(po["acc"], EXP * pair + e - 1)
                    V.scalar_tensor_tensor(prod[:, e % 2, :], YB[e % 2][:, 0:TT], eb2[:, e:e + 1],
                                           gateB[:, e, :], ALU.add, ALU.mult).then_inc(ve_s["prod"], 1)
                if n == FINISH:
                    dv.wait_ge(pe["out"], pair + 1)
                    dv.wait_ge(out_free, pair + 1)
                    V.tensor_tensor(outb[:, :, :].rearrange("p (h i) f -> p i h f", h=G),
                                    YB[0][0:TP, 0:NT * 128].rearrange("p (i h f) -> p i h f", i=NT, h=G),
                                    res[3][:, :, :].rearrange("p (h i) f -> p i h f", h=G),
                                    ALU.add).then_inc(ve_s["out"], 1)

            def none(pair):
                pass

            front = [conv, combine, none, none, scores_a, scores_b, pv, none, router, none, ffn_down, none, none,
                     usum, denoms, gram, linear, none, dy, embed, none, route]

            V.memset(mhalf[:, :], -0.5)
            V.memset(seen[:, 0:4], 0.0)
            V.memset(grown[:, 0:1], 0.0)
            V.memset(gsT[:, TT:TW].bitcast(f32), 0.0)
            V.memset(x5T[:, :, TT:TW].bitcast(f32), 0.0)
            V.memset(probs[:, :, T:TT], 0.0).then_inc(cst_set, 1)
            dv.wait_ge(pack_in[0], 16)
            conv(0)
            combine(0)
            dv.wait_ge(pack_in[1], 16)
            dv.wait_ge(cst_set, 1)
            for stage in front[2:7]:
                stage(0)
            dv.wait_ge(pack_in[2], 16)
            dv.wait_ge(pack_in[3], 16)
            V.tensor_tensor(w1g[:, :, :], w1, gT.unsqueeze(2).to_broadcast([128, EXP, H]),
                            ALU.mult).then_inc(w1g_set, 1)
            dv.wait_ge(w1g_set, 1)
            V.tensor_copy(w1s[:, 0, :, :], w1g[:, :, :]).then_inc(w1hi_set, 1)
            dv.wait_ge(w1hi_set, 1)
            V.tensor_tensor(w1s[:, 1, :, :], w1g[:, :, :], w1s[:, 0, :, :].bitcast(f32),
                            ALU.subtract).then_inc(w1s_set, 1)
            dv.wait_ge(b1f_mm, 1)
            V.tensor_tensor(b1f[:, :], HB[1][:, 0:EXP * HC], b1, ALU.add).then_inc(b1f_set, 1)
            for stage in front[7:]:
                stage(0)
            with dv.Fori(0, NP - 1) as pair:
                for n, stage in enumerate(front):
                    stage(pair + 1)
                    experts(pair, n)
            for n in range(FINISH + 1):
                experts(NP - 1, n)

        @block.gpsimd
        def _(gp):
            P = nc.gpsimd

            def root(n, pair):
                gp.wait_ge(ln_mv[n], pair + 1)
                gp.nop(nofuse=True)
                P.tensor_scalar(ve[n][:, :], mv[n][:, :, 1], LN_EPS, 1.0, ALU.add, ALU.mult).then_inc(ln_ve[n], 1)
                gp.wait_ge(ln_ve[n], pair + 1)
                P.tensor_tensor(rstd[n][:, :], ve[n][:, :], mhalf[0:TP, :], ALU.pow).then_inc(ln_rs[n], 1)

            def scaled_root(n, pair):
                gp.wait_ge(ln_mv[n], pair + 1)
                gp.wait_ge(ve_s["rsq"], pair + 1)
                P.tensor_tensor(ve[n][:, :], mv[n][:, :, 1], rsq[:, :], ALU.mult).then_inc(ln_ve[n], 1)
                gp.wait_ge(ln_ve[n], 3 * pair + 1)
                gp.nop(nofuse=True)
                P.tensor_scalar(vra[:, :], ve[n][:, :], LN_EPS, 1.0, ALU.add, ALU.mult).then_inc(ln_ve[n], 1)
                gp.wait_ge(ln_ve[n], 3 * pair + 2)
                P.tensor_tensor(vrb[:, :], vra[:, :], mhalf[0:TP, :], ALU.pow).then_inc(ln_ve[n], 1)
                gp.wait_ge(ln_ve[n], 3 * pair + 3)
                P.tensor_tensor(rstd[n][:, :], vrb[:, :], rt[:, :], ALU.mult).then_inc(ln_rs[n], 1)

            def combine(pair):
                gp.wait_ge(ve_s["wn"], pair + 1)
                P.tensor_tensor(wr[:, :], wn[:, :], mhalf[0:TP, :], ALU.pow).then_inc(po["wr"], 1)
                gp.wait_ge(po["wr"], pair + 1)
                gp.nop(nofuse=True)
                P.tensor_scalar(cs_scale[:, :], wr[:, :], cscale[0:TP, 0:1], 1.0, ALU.mult,
                                ALU.mult).then_inc(po["scale"], 1)
                root(0, pair)

            def pv(pair):
                root(1, pair)
                gp.wait_ge(ln_xn[1], G * pair + G)
                P.tensor_tensor(hx[:, :, :], res[1][:, :, :], xn[1][:, :, :], ALU.add).then_inc(po["hx"], 1)

            def ffn_down(pair):
                root(2, pair)
                root_again("var3", "again3", pair)

            def root_again(var, done, pair):
                gp.wait_ge(ve_s[var], 2 * pair + 2)
                gp.nop(nofuse=True)
                P.tensor_scalar(vra[:, :], twice[:, :], LN_EPS, 1.0, ALU.add, ALU.mult).then_inc(po[done], 1)
                gp.wait_ge(po[done], 2 * pair + 1)
                P.tensor_tensor(again[:, :], vra[:, :], mhalf[0:TP, :], ALU.pow).then_inc(po[done], 1)
                gp.wait_ge(po[done], 2 * pair + 2)

            def denoms(pair):
                gp.wait_ge(ac["u"], HC * G * pair + HC * G)
                gp.nop(nofuse=True)
                P.tensor_copy(z[:, :, :, 0:1], u[:, :, :, 0:1]).then_inc(po["z0"], 1)
                gp.wait_ge(ve_s["rt"], pair + 1)
                P.tensor_tensor(vrb[:, :], again[:, :], rt[:, :], ALU.mult).then_inc(po["lnvr"], 1)
                gp.wait_ge(ln_xn[2], G * pair + G)
                gp.wait_ge(po["lnvr"], 2 * pair + 1)
                P.tensor_tensor(lnvr[:, :, :], xn[2][:, :, :], vrb[:, :].unsqueeze(2).to_broadcast([TP, Q, D]),
                                ALU.mult).then_inc(po["lnvr"], 1)

            def linear(pair):
                scaled_root(4, pair)

            def embed(pair):
                scaled_root(5, pair)
                root(6, pair)
                root_again("var7", "again7", pair)
                P.tensor_tensor(lnsc[:, :], again[:, :], rstd[6][:, :], ALU.mult).then_inc(po["lnsc"], 1)
                P.tensor_tensor(unagain[:, :], again[:, :], vra[:, :], ALU.mult).then_inc(po["unagain"], 1)

            def none(pair):
                pass

            def experts(pair, n):
                e = n // G - 1
                if not (n % G == 0 and 0 <= e < EXP):
                    return
                gp.wait_ge(ve_s["prod"], EXP * pair + e + 1)
                if e == 0:
                    gp.nop(nofuse=True)
                    P.tensor_copy(acc[:, 1, :], prod[:, 0, :]).then_inc(po["acc"], 1)
                else:
                    gp.wait_ge(po["acc"], EXP * pair + e)
                    P.tensor_tensor(acc[:, (e + 1) % 2, :], acc[:, e % 2, :], prod[:, e % 2, :],
                                    ALU.add).then_inc(po["acc"], 1)

            front = [none, combine, none, none, none, none, pv, none, none, none, ffn_down, none, none,
                     none, denoms, none, linear, none, none, embed, none, none]
            gp.wait_ge(cst_set, 1)
            gp.wait_ge(pack_in[0], 16)
            for stage in front:
                stage(0)
            with gp.Fori(0, NP - 1) as pair:
                for n, stage in enumerate(front):
                    stage(pair + 1)
                    experts(pair, n)
            for n in range(FINISH + 1):
                experts(NP - 1, n)


def kernel(**inputs):
    import numpy as _np
    import concourse.bacc as _bacc
    from concourse import mybir as _mybir
    from concourse.bass_utils import run_bass_kernel_spmd as _run

    a = {k: _np.asarray(v) for k, v in inputs.items()}
    f = _np.float32
    x = a["x"]
    x_T = _np.zeros((CIN, B, XC), f)
    x_T[:, :, 0:L] = x.transpose(2, 0, 1)
    x_nat = _np.ascontiguousarray(x.reshape(B, XP, XJ, CIN).transpose(1, 0, 2, 3))

    def rows(v, n=128):
        return _np.broadcast_to(v.reshape(1, -1), (n, v.size))

    def halves(w):
        return w.reshape(HC, 128, -1).transpose(1, 0, 2).reshape(128, -1)

    t = _np.arange(TT)
    band = _np.zeros((XP, XJ, TT), f)
    for j in range(XJ):
        d = XJ * _np.arange(XP)[:, None] + j - t[None, :]
        band[:, j] = (d >= 0) & (d < KW)
    smask = _np.concatenate([_np.where(t[None, :SW[i]] < (TP * i + _np.arange(TP))[:, None], 0.0, NEG)
                             for i in range(NT)], axis=1)
    rankc = _np.stack([_np.where(t[None, :T] < (TP * i + _np.arange(TP))[:, None], 0.0, TINY)
                       for i in range(NT)], axis=1)
    decay = []
    for i in range(NT):
        d = t[None, TP * i:] - (TP * i + _np.arange(TP))[:, None] - 1
        decay.append(_np.where(d >= 0, DECAY ** _np.maximum(d, 0).astype(_np.float64), 0.0))
    e = _np.arange(EXP)
    topc = _np.where(e[None, :] < e[:, None], 0.0, TINY)
    pick = _np.zeros((128, G, G), f)
    pick[:, range(G), range(G)] = 1.0
    pick = pick.reshape(128, -1)
    spread = _np.zeros((2, G, EXP, EXP, G, D), f)
    for h in range(G):
        spread[:, h, range(EXP), range(EXP), h, :] = 1.0
    spread = spread.reshape(2 * G * EXP, -1)

    values = {
        "conv": a["L0_tok_kernel"].transpose(1, 0, 2).reshape(CIN, KW * D),
        "eye2": _np.concatenate([_np.eye(D), _np.eye(D)]), "band": band.reshape(XP, -1),
        "cbias": rows(a["L0_tok_bias"]), "cscale": rows(a["L0_tok_scale"]),
        "ident": _np.eye(128), "wq": a["L0_attn_Wq"], "wk": a["L0_attn_Wk"], "wvT": a["L0_attn_Wv"].T,
        "smask": smask, "wrB": _np.broadcast_to(a["L0_ffn_wr"], (D, TP)), "brB": rows(a["L0_ffn_br"]),
        "rankc": rankc.reshape(TP, -1), "fw1": a["L0_ffn_w1"], "fb1": a["L0_ffn_b1"].reshape(HC, 128).T,
        "fw2": halves(a["L0_ffn_w2"]), "fb2": rows(a["L0_ffn_b2"]),
        "dxT": a["L1_attn_Dx"].T, "ones": _np.ones((128, 128)), "decay": _np.concatenate(decay, axis=1),
        "dyT": a["L1_attn_Dy"].T, "eT": halves(a["L1_attn_E"].T), "rw": _np.concatenate([a["L1_ffn_Wr"]] * 2),
        "rb": rows(a["L1_ffn_br"]), "topc": rows(topc), "pick": pick, "spread": spread,
        "eb2": _np.concatenate([a["L1_ffn_b2"].T] * G),
        "w1": _np.concatenate([a["L1_ffn_W1"].transpose(1, 0, 2).reshape(D, -1)] * 2),
        "gT": _np.concatenate([a["L1_ffn_ln_g"].T] * 2),
        "bT": a["L1_ffn_ln_b"].T, "b1": a["L1_ffn_b1"].reshape(EXP * HC, 128).T,
        "w2": a["L1_ffn_W2"].reshape(EXP * HC, 128, D).transpose(1, 0, 2).reshape(128, -1),
    }
    at, widths = fields()
    packs = [_np.zeros((128, w), f) for w in widths]
    for name, v in values.items():
        n, c, cols, nrows = at[name]
        packs[n][0:nrows, c:c + v.shape[1]] = v

    nc = _bacc.Bacc("TRN2", target_bir_lowering=False, num_devices=1)
    arrays = {"in_x_nat": x_nat, "in_x_T": x_T} | {f"in_pack{n}": p for n, p in enumerate(packs)}
    aps = {n: nc.dram_tensor(n, v.shape, _mybir.dt.from_np(v.dtype), kind="ExternalInput").ap()
           for n, v in arrays.items()}
    out = nc.dram_tensor("out_0_dram", (TP, B * NT, D), _mybir.dt.float32, kind="ExternalOutput").ap()
    build(nc, aps["in_x_nat"], aps["in_x_T"], [aps[f"in_pack{n}"] for n in range(len(packs))], out)
    r = _run(nc, [arrays], core_ids=[0])
    got = r.results[0]["out_0_dram"]
    return _np.ascontiguousarray(
        got.reshape(TP, B, NT, D).transpose(1, 2, 0, 3).reshape(B, TT, D)[:, :T])
```

```python
import numpy as np

import concourse.bass as bass
from concourse import mybir
from contextlib import ExitStack

B, L, CIN, KW, D = 8, 375, 128, 15, 64
T = L - KW + 1
TP, NT = 121, 3
TT = TP * NT
XC = 2 * (KW // 2) + TT + 1
XP, XJ = 125, 3
G = 2
NP = B // G
Q = G * NT
H = 256
HC = H // 128
EXP, TOPK = 8, 2
KEEP = max(1, T // 2) - 1
DECAY = 0.97
TAPS = (KW + 1) // 2
UNITS = EXP * G
TW = TT + 1
NEG = -1.0e10
TINY = float(np.finfo(np.float32).tiny)
SW = [T, 2 * TP, T]


def fields():
    groups = [
        [("conv", 2 * TAPS * D, CIN), ("eye2", D, 128), ("band", XJ * TT, XP), ("cbias", D, 128),
         ("cscale", 1, 128)],
        [("ident", 128, 128), ("wq", D, D), ("wk", D, D), ("wvT", D, 128), ("smask", sum(SW), TP),
         ("wrB", TP, 128), ("brB", 1, 128)],
        [("rankc", NT * T, TP), ("fw1", H, 128), ("fb1", HC, 128), ("fw2", HC * D, 128), ("fb2", 1, 128),
         ("dxT", H, 128), ("ones", 128, 128), ("decay", 2 * TT, TP), ("dyT", H, 128), ("eT", HC * D, 128),
         ("rw", EXP, 128), ("rb", EXP, 128), ("topc", EXP * EXP, 128), ("pick", G * G, 128),
         ("spread", EXP * 128, 2 * G * EXP)],
        [("w1", EXP * H, 128), ("gT", EXP, 128), ("bT", EXP, D), ("b1", EXP * HC, 128), ("eb2", EXP, 128),
         ("w2", EXP * HC * D, 128)],
    ]
    at = {}
    for n, group in enumerate(groups):
        c = 0
        for name, cols, rows in group:
            at[name] = (n, c, cols, rows)
            c += cols
    return at, [sum(g[1] for g in group) for group in groups]


def build(nc, x_nat, x_T, packs, out):
    f32 = mybir.dt.float32
    f32r = mybir.dt.float32r
    ALU = mybir.AluOpType
    ACT = mybir.ActivationFunctionType
    AX = mybir.AxisListType
    at, widths = fields()

    ctx = ExitStack()
    with ctx:
        def sb(name, shape, dt=f32):
            return ctx.enter_context(nc.sbuf_tensor(name, shape, dt))

        def sem(name):
            return ctx.enter_context(nc.semaphore(name))

        pack_sb = [sb(f"pack{n}", [128, w]) for n, w in enumerate(widths)]

        def field(name):
            n, c, cols, rows = at[name]
            return pack_sb[n][0:rows, c:c + cols]

        conv_w, eye2, cbias, cscale = field("conv"), field("eye2"), field("cbias"), field("cscale")
        band = field("band").rearrange("p (j t) -> p j t", j=XJ)
        ident, wq, wk, wvT, smask = (field(n) for n in ("ident", "wq", "wk", "wvT", "smask"))
        wrB, brB = field("wrB"), field("brB")
        rankc = field("rankc").rearrange("p (i t) -> p i t", i=NT)
        fw1, fb1, fb2 = field("fw1"), field("fb1"), field("fb2")
        fw2 = field("fw2").rearrange("p (c f) -> p c f", c=HC)
        dxT, dyT, ones, decay = field("dxT"), field("dyT"), field("ones"), field("decay")
        eT = field("eT").rearrange("p (c f) -> p c f", c=HC)
        rw, rb, eb2 = field("rw"), field("rb"), field("eb2")
        pick = field("pick").rearrange("p (h m) -> p h m", h=G)
        topc = field("topc").rearrange("p (e f) -> p e f", e=EXP)
        w1 = field("w1").rearrange("p (e n) -> p e n", e=EXP)
        gT, bT, b1 = field("gT"), field("bT"), field("b1")
        w2 = field("w2").rearrange("p (u f) -> p u f", f=D)

        wqk = sb("wqk", [128, D])
        w1s = sb("w1s", [128, 2, EXP, H], f32r)
        spread = sb("spread", [2 * G * EXP, EXP, 128], f32r)
        b1f = sb("b1f", [128, EXP * HC])
        mhalf = sb("mhalf", [128, Q])

        xnat = sb("xnat", [XP, G, XJ, CIN])
        sq = sb("sq", [XP, G * XJ])
        wn = sb("wn", [TP, Q])
        wr = sb("wr", [TP, Q])
        cs_scale = sb("cs_scale", [TP, Q])
        res = [sb(f"res{n}", [TP, Q, D]) for n in range(4)]
        LN = (0, 1, 2, 4, 5, 6)
        PHASE = {n: "A" if n < 3 else "B" for n in LN}
        xn = {n: sb(f"xn{n}", [TP, Q, D]) for n in LN if n != 6}
        stats = {n: sb(f"stats{n}", [TP, Q, 6]) for n in LN}
        mv = {n: sb(f"mv{n}", [TP, Q, 2]) for n in LN}
        ve = {n: sb(f"ve{n}", [TP, Q]) for n in LN}
        rstd = {n: sb(f"rstd{n}", [TP, Q]) for n in LN}
        xc = {k: sb("xc" + k, [TP, Q, D]) for k in "AB"}
        probs = sb("probs", [TP, Q, TT])
        smax = sb("smax", [TP, Q])
        nmax = sb("nmax", [TP, Q])
        ssum = sb("ssum", [TP, Q])
        rsum = sb("rsum", [TP, Q])
        vv = sb("vv", [TP, Q, D])
        wB = sb("wB", [TP, G, T])
        ranks = probs
        crow = sb("crow", [TP, Q])
        cdiag = sb("cdiag", [TP, Q, TP])
        twice = {n: sb(f"twice{n}", [TP, Q]) for n in (2, 6)}
        vrt = {n: sb(f"vrt{n}", [TP, Q]) for n in (2, 6)}
        again = {n: sb(f"again{n}", [TP, Q]) for n in (2, 6)}
        unagain = sb("unagain", [TP, Q])
        lnsc = sb("lnsc", [TP, Q])
        wcol = sb("wcol", [TP, Q])
        rank = sb("rank", [TP, Q])
        mw = sb("mw", [TP, Q])
        hx = sb("hx", [TP, Q, D])
        fy = sb("fy", [TP, Q, D])
        rt = sb("rt", [TP, Q])
        rsq = sb("rsq", [TP, Q])
        vra = sb("vra", [TP, Q])
        vrb = sb("vrb", [TP, Q])
        vrc = sb("vrc", [TP, Q])
        lnvr = sb("lnvr", [TP, Q, D])
        gd = sb("gd", [TP, G, 2 * TT])
        lg = sb("lg", [TP, Q, EXP])
        lmax = sb("lmax", [TP, Q])
        ex = sb("ex", [TP, Q, EXP])
        dif = sb("dif", [TP, Q, EXP, EXP])
        erank = sb("erank", [TP, Q, EXP])
        esel = sb("esel", [TP, Q, EXP])
        eden = sb("eden", [TP, Q])
        xT = sb("xT", [CIN, G, XC])
        cs = sb("cs", [128, G, TT])
        xnT = sb("xnT", [128, TT])
        attT = sb("attT", [128, TT])
        fyT = attT
        v_starT = sb("v_starT", [128, TT])
        gq = sb("gq", [128, TT])
        x2T = sb("x2T", [128, TT])
        hT = sb("hT", [128, G, HC, TT])
        vT = sb("vT", [128, TT])
        u = sb("u", [128, G, HC, TT])
        us = sb("us", [G, TT])
        ub = sb("ub", [G, TT])
        seen = sb("seen", [G, TT + 4])
        grow = sb("grow", [G, TT])
        fed = sb("fed", [G, TT])
        grown = sb("grown", [G, TT + 1])
        den = sb("den", [G, TT])
        den2 = sb("den2", [G, TT])
        z = sb("z", [128, G, HC, TT])
        naT = sb("naT", [128, TT])
        yT = sb("yT", [128, G, HC, TT])
        x5 = sb("x5", [TP, Q, D])
        x5s = sb("x5s", [TP, Q, 2, D], f32r)
        x5N = sb("x5N", [128, G, TW], f32r)
        x5T = sb("x5T", [128, G, TW], f32r)
        gate = sb("gate", [TP, NT, G, EXP])
        gates = sb("gates", [TP, NT, 2, G, EXP], f32r)
        gsT = sb("gsT", [2 * G * EXP, TW], f32r)
        gateB = sb("gateB", [128, EXP, TT])
        hid = sb("hid", [128, 2, G, HC, TT])
        w1g = hid[:, :, 0, 0, 0:H]
        prod = sb("prod", [128, 2, TT])
        acc = sb("acc", [128, 2, TT])
        keep = sb("keep", [TP, Q, D])
        outb = sb("outb", [TP, Q, D])

        AB = [ctx.enter_context(nc.psum_tensor(f"AB{h}", [128, 512], f32)) for h in range(2)]
        BB = [ctx.enter_context(nc.psum_tensor(f"BB{h}", [128, 512], f32)) for h in range(3)]
        HB = [ctx.enter_context(nc.psum_tensor(f"HB{h}", [128, 512], f32)) for h in range(HC)]
        YB = ctx.enter_context(nc.psum_tensor("YB", [128, 512], f32))

        DX_BANK, GRAM_BANK = [BB[2], BB[0], BB[1], BB[2]], [BB[1], BB[0], BB[2], BB[1]]
        GATE_BANK = [BB[(2 + e) % 3] for e in range(EXP)]

        x_in, pack_in, out_st = sem("x_in"), [sem(f"pack_in{n}") for n in range(len(widths))], sem("out_st")
        out_free = sem("out_free")
        cst_set, wqk_mm, wqk_set, w1g_set, w1hi_set, w1s_set, spread_set, b1f_mm, b1f_set = (sem(n) for n in (
            "cst_set", "wqk_mm", "wqk_set", "w1g_set", "w1hi_set", "w1s_set", "spread_set", "b1f_mm", "b1f_set"))
        pe = {n: sem("pe_" + n) for n in (
            "conv", "comb", "win", "t1", "proj", "sc", "v", "pv", "t2", "rt", "f1", "f2", "fb", "t3", "dx",
            "usum", "denT", "carry", "gram", "a", "t4", "dy", "e", "eb", "t5", "lg", "gT", "gB", "w1", "y", "out")}
        ac = {n: sem("act_" + n) for n in (
            "sq", "cslo", "xnT", "gq", "exp", "attT", "fyT", "vstT", "x2T", "hT", "vT", "u", "us", "naT", "x5N", "x5hi", "ex", "gsT",
            "gB", "hid")}
        ve_s = {n: sem("dve_" + n) for n in (
            "cshi", "wn", "res0", "sc", "nmax", "rsum", "vv", "res1", "wB", "wcol", "rank", "mw", "fy",
            "res2", "var3", "var7", "seen", "ub", "grow", "fed", "grown", "den", "guard", "crow", "cdiag",
            "z", "rt", "rsq", "gd", "yT", "res3", "x5", "x5lo", "lg", "lb", "lmax", "lsub", "dif", "cmp",
            "erank", "esel", "eden", "erec", "gate", "ghi", "glo", "prod", "out")}
        po = {n: sem("pool_" + n) for n in (
            "wr", "scale", "hx", "again3", "again7", "unagain", "z0", "lnsc", "lnvr", "keep", "x5T", "acc")}
        ln_st = {k: sem("ln_st" + k) for k in "AB"}
        ln_mv = {n: sem(f"ln_mv{n}") for n in LN}
        ln_ve = {n: sem(f"ln_ve{n}") for n in LN}
        ln_rs = {n: sem(f"ln_rs{n}") for n in LN}
        ln_xc = {k: sem("ln_xc" + k) for k in "AB"}
        ln_xn = {n: sem(f"ln_xn{n}") for n in LN}
        LN_EPS = 1e-5

        SCHEDULE = """A.win B.t3 A.conv0 B.dx X0 B.usum X1 A.conv1 X2 B.denoms Y0 X3 Z0 B.carry Y1 A.combine X4 B.gram
            X5 Z1 A.norm0 B.linear A.t1 X6 Y2 B.norm4 X7 A.proj X8 B.t4 X9 Z2 A.scores A.exp B.dy Y3 Z3
            A.values B.embed B.eback A.pv X10 B.norm5 B.twice6 Y4 A.v X11 X12 Z4 B.x5 A.norm1 X13 B.split
            X14 Y5 Z5 B.t5 A.t2 B.logits Y6 B.ex Z6 A.router A.ffn_up A.rank B.gate X15 A.ffn_down Y7 Z7
            A.fback A.norm2 B.gates XF""".split()
        RAMP = """X0 X1 A.win X2 X3 X4 A.conv0 B.t3 A.conv1 B.dx A.combine A.norm0 B.usum X5 A.t1 A.proj B.denoms
            A.scores A.exp Y0 B.carry X6 X7 A.values B.gram B.linear A.pv X8 X9 B.norm4 B.t4 Y1 A.v Y2 Y3
            X10 B.dy A.norm1 Z0 Z1 B.embed Z2 X11 Z3 A.t2 Y4 B.eback A.router B.norm5 X12 B.twice6 Y5
            A.ffn_up B.x5 X13 Z4 B.split Y6 A.rank B.t5 X14 B.logits X15 Z5 B.ex Z6 Y7 Z7 B.gate A.ffn_down
            A.fback A.norm2 XF B.gates""".split()
        DRAIN = """B.t3 B.dx X0 B.usum X1 X2 Y0 Z0 X3 B.denoms X4 Y1 B.carry B.gram B.linear X5 Z1 X6 B.norm4 Y2 X7
            Z2 B.t4 X8 B.dy X9 B.embed Y3 Z3 B.eback X10 Y4 Z4 B.norm5 B.twice6 X11 X12 Y5 X13 X14 Z5 Y6
            B.x5 B.split X15 Z6 B.t5 B.logits Y7 B.ex Z7 B.gate XF B.gates""".split()

        def run(stages, experts, a=None, b=None, x=None, order=SCHEDULE):
            for name in order:
                if name[0] in "XYZ":
                    if x is not None:
                        experts(x, name)
                elif name in stages:
                    pair = a if name[0] == "A" else b
                    if pair is not None:
                        stages[name](pair)

        def ln_count(n, pair):
            return 3 * pair + (n + 1 if n < 3 else n - 3)

        block = ctx.enter_context(nc.Block())

        def rows_of(h):
            return slice(D * h, D * (h + 1))

        def tile_q(h, i):
            return G * i + h

        @block.sync
        def _(sp):
            def load_x(pair, later=True):
                if later:
                    sp.wait_ge(pe["conv"], G * pair)
                    sp.wait_ge(ac["sq"], pair)
                sp.dma_start(xT[:, :, :], x_T[:, bass.ds(pair * G, G), :]).then_inc(x_in, 16)
                sp.dma_start(xnat[:, :, :, :], x_nat[:, bass.ds(pair * G, G), :, :]).then_inc(x_in, 16)

            def store(pair):
                sp.wait_ge(ve_s["out"], pair + 1)
                sp.dma_start(out[:, bass.ds(pair * Q, Q), :], outb[:, :, :]).then_inc(out_st, 16)
                sp.wait_ge(out_st, 16 * pair + 16)
                sp.sem_inc(out_free, 1)

            sp.dma_start(pack_sb[0][:, :], packs[0]).then_inc(pack_in[0], 16)
            sp.sem_inc(out_free, 1)
            load_x(0, later=False)
            for n in range(1, len(widths)):
                sp.dma_start(pack_sb[n][:, :], packs[n]).then_inc(pack_in[n], 16)
            load_x(1)
            load_x(2)
            with sp.Fori(0, NP - 3) as pair:
                load_x(pair + 3)
                store(pair)
            for pair in range(NP - 3, NP - 1):
                store(pair)
            store(NP - 1)

        @block.tensor
        def _(te):
            mm = nc.tensor.matmul

            def tok(i):
                return slice(TP * i, TP * (i + 1))

            def transposes(dst, src, done):
                te.nop(nofuse=True)
                for i in range(NT):
                    last = nc.tensor.transpose(dst[:, tok(i)], src[:, G * i:G * (i + 1), :].rearrange("p h f -> p (h f)"),
                                               ident[0:TP, 0:TP])
                last.then_inc(done, 1)

            def back(dst, src, done):
                te.nop(nofuse=True)
                for i in range(NT):
                    last = nc.tensor.transpose(dst[0:TP, 128 * i:128 * (i + 1)], src[:, tok(i)], ident)
                last.then_inc(done, 1)

            def to_hidden(w, src, h, c, dst):
                return mm(dst[:, 0:TT], w[rows_of(h), 128 * c:128 * (c + 1)], src[rows_of(h), :], start=True, stop=True)

            def from_hidden(src, w, dst):
                for c in range(HC):
                    for h in range(G):
                        last = mm(dst[rows_of(h), 0:TT], w[:, c, :], src[:, h, c, :], start=(c == 0), stop=(c == HC - 1))
                return last

            def win(pair):
                if not (isinstance(pair, int) and pair == 0):
                    te.wait_ge(ve_s["fy"], pair)
                te.wait_ge(ac["sq"], pair + 1)
                for i in range(NT):
                    for j in range(XJ):
                        last = mm(AB[1][0:TP, G * i:G * (i + 1)], band[:, j, tok(i)], sq[:, j::XJ],
                                  start=(j == 0), stop=(j == XJ - 1))
                last.then_inc(pe["win"], 1)

            def conv(h, pair):
                te.wait_ge(x_in, 32 * (pair + 1))
                if h == 1:
                    te.wait_ge(ve_s["wn"], pair + 1)
                for k in range(TAPS):
                    last = mm(AB[h][:, 0:TT + 1], conv_w[:, 2 * D * k:2 * D * (k + 1)],
                              xT[:, h, 2 * k:2 * k + TT + 1], start=(k == 0), stop=(k == TAPS - 1))
                last.then_inc(pe["conv"], 1)

            def conv0(pair):
                conv(0, pair)

            def conv1(pair):
                conv(1, pair)

            def combine(pair):
                for h in range(G):
                    te.wait_ge(ac["cslo"], G * pair + h + 1)
                    te.wait_ge(ve_s["cshi"], G * pair + h + 1)
                    for i in range(NT):
                        q = tile_q(h, i)
                        last = mm(AB[0][0:TP, D * q:D * (q + 1)], cs[:, h, tok(i)], eye2, start=True, stop=True)
                last.then_inc(pe["comb"], 1)

            def t1(pair):
                te.wait_ge(ln_xn[0], pair + 1)
                transposes(AB[0], xn[0], pe["t1"])

            def proj(pair):
                te.wait_ge(ac["xnT"], pair + 1)
                te.nop(nofuse=True)
                for h in range(G):
                    last = mm(AB[1][rows_of(h), 0:TT], wqk[rows_of(h), :], xnT[rows_of(h), :], start=True, stop=True)
                last.then_inc(pe["proj"], 1)

            def scores(pair):
                te.wait_ge(ac["gq"], pair + 1)
                for s in range(Q):
                    h, n = s // NT, s % NT
                    if s >= 2:
                        te.wait_ge(ve_s["sc"], Q * pair + s - 1)
                    mm(AB[s % 2][0:TP, 0:SW[n]], xnT[rows_of(h), tok(n)], gq[rows_of(h), 0:SW[n]],
                       start=True, stop=True).then_inc(pe["sc"], 1)

            def pv(pair):
                te.wait_ge(ve_s["vv"], pair + 1)
                for k, queries in enumerate((TT, SW[1], TT)):
                    for h in range(G):
                        keys = min(TP, T - TP * k)
                        last = mm(AB[0][rows_of(h), 0:queries], vv[0:keys, tile_q(h, k), :],
                                  probs[0:keys, tile_q(h, k), 0:queries], start=(k == 0), stop=(k == NT - 1))
                last.then_inc(pe["pv"], 1)

            def values(pair):
                te.wait_ge(ac["attT"], pair + 1)
                for i in range(NT):
                    for h in range(G):
                        last = mm(AB[h][0:TP, D * i:D * (i + 1)], attT[rows_of(h), tok(i)], wvT[rows_of(h), :],
                                  start=True, stop=True)
                last.then_inc(pe["v"], 1)

            def t2(pair):
                te.wait_ge(ln_xn[1], pair + 1)
                transposes(AB[0], xn[1], pe["t2"])

            def router(pair):
                te.wait_ge(ac["x2T"], pair + 1)
                for h in range(G):
                    mm(AB[h][0:TP, 0:T], wrB[rows_of(h), :], x2T[rows_of(h), 0:T], start=True,
                       stop=True).then_inc(pe["rt"], 1)

            def ffn_up(pair):
                for n in range(HC * G):
                    c, h = n // G, n % G
                    if n < G:
                        te.wait_ge(ve_s["wB"], G * pair + h + 1)
                    else:
                        te.wait_ge(ac["hT"], HC * G * pair + n - G + 1)
                    to_hidden(fw1, x2T, h, c, AB[h]).then_inc(pe["f1"], 1)

            def ffn_down(pair):
                te.wait_ge(ac["hT"], HC * G * pair + HC * G)
                from_hidden(hT, fw2, AB[0]).then_inc(pe["f2"], 1)

            def fback(pair):
                te.wait_ge(ac["fyT"], pair + 1)
                back(AB[1], fyT, pe["fb"])

            def t3(pair):
                if not (isinstance(pair, int) and pair == 0):
                    te.wait_ge(ac["gB"], EXP * pair)
                te.wait_ge(ln_xn[2], pair + 1)
                transposes(BB[0], xn[2], pe["t3"])

            def dx(pair):
                te.wait_ge(ac["vT"], pair + 1)
                for n in range(HC * G):
                    h, c = n // HC, n % HC
                    if n == 3:
                        te.wait_ge(ac["u"], HC * G * pair + 1)
                    to_hidden(dxT, vT, h, c, DX_BANK[n]).then_inc(pe["dx"], 1)

            def usum(pair):
                te.wait_ge(ac["u"], HC * G * pair + HC * G)
                for n in range(HC * G):
                    last = mm(BB[0][0:G, 0:TT], pick[:, n // HC, :], u[:, n // HC, n % HC, :],
                              start=(n == 0), stop=(n == HC * G - 1))
                last.then_inc(pe["usum"], 1)

            def denoms(pair):
                te.wait_ge(ve_s["guard"], pair + 1)
                te.nop(nofuse=True)
                for i in range(NT):
                    last = nc.tensor.transpose(BB[1][0:TP, G * i:G * (i + 1)], den2[:, tok(i)], ident[0:G, 0:G])
                last.then_inc(pe["denT"], 1)

            def carry(pair):
                te.wait_ge(ve_s["cdiag"], pair + 1)
                for h in range(G):
                    mm(BB[2 * h][:, 0:TT], ones[0:TP, :], cdiag[:, h::G, :],
                       start=True, stop=True).then_inc(pe["carry"], 1)

            def gram(pair):
                te.wait_ge(po["z0"], pair + 1)
                for n in range(2 * G):
                    h = n // 2
                    te.wait_ge(ve_s["z"], G * pair + h + 1)
                    if n == 3:
                        te.wait_ge(ve_s["gd"], 2 * G * pair + 1)
                    at_col = 0
                    for i in ((0,), (1, 2))[n % 2]:
                        w = TT - TP * i
                        for c in range(HC):
                            last = mm(GRAM_BANK[n][0:TP, at_col:at_col + w], z[:, h, c, tok(i)],
                                      z[:, h, c, TP * i:TT], start=(c == 0), stop=(c == HC - 1))
                        at_col += w
                    last.then_inc(pe["gram"], 1)

            def linear(pair):
                te.wait_ge(po["lnvr"], 2 * pair + 2)
                for h in range(G):
                    te.wait_ge(ve_s["gd"], 2 * (G * pair + h) + 2)
                    for k in range(NT):
                        for i in range(k + 1):
                            first = (0, TT, TT + 2 * TP)[i] + TP * (k - i)
                            last = mm(BB[0][0:TP, D * tile_q(h, k):D * (tile_q(h, k) + 1)],
                                      gd[:, h, first:first + TP], lnvr[:, tile_q(h, i), :],
                                      start=(i == 0), stop=(i == k))
                last.then_inc(pe["a"], 1)

            def t4(pair):
                te.wait_ge(ln_xn[4], pair + 1)
                transposes(BB[0], xn[4], pe["t4"])

            def dy(pair):
                te.wait_ge(ac["naT"], pair + 1)
                for n in range(HC * G):
                    h, c = n // HC, n % HC
                    if n == 3:
                        te.wait_ge(ve_s["yT"], HC * G * pair + 1)
                    to_hidden(dyT, naT, h, c, DX_BANK[n]).then_inc(pe["dy"], 1)

            def embed(pair):
                te.wait_ge(ve_s["yT"], HC * G * pair + HC * G)
                from_hidden(yT, eT, BB[0]).then_inc(pe["e"], 1)

            def eback(pair):
                te.wait_ge(ac["vstT"], pair + 1)
                back(BB[1], v_starT, pe["eb"])

            def t5(pair):
                te.wait_ge(ac["x5hi"], pair + 1)
                te.wait_ge(ve_s["x5lo"], pair + 1)
                for h in range(G):
                    te.nop(nofuse=True)
                    for i in range(NT):
                        last = nc.tensor.transpose(
                            BB[1 + h][:, tok(i)], x5s[:, tile_q(h, i), :, :].rearrange("p s f -> p (s f)").bitcast(f32),
                            ident[0:TP, 0:TP])
                    last.then_inc(pe["t5"], 1)

            def logits(pair):
                for h in range(G):
                    te.wait_ge(ac["x5N"], G * pair + h + 1)
                    for i in range(NT):
                        q = tile_q(h, i)
                        last = mm(BB[0][0:TP, EXP * q:EXP * (q + 1)], x5N[:, h, tok(i)].bitcast(f32), rw,
                                  start=True, stop=True)
                last.then_inc(pe["lg"], 1)

            def gates_out(pair):
                te.wait_ge(ve_s["glo"], pair + 1)
                te.wait_ge(ve_s["ghi"], pair + 1)
                te.nop(nofuse=True)
                for i in range(NT):
                    last = nc.tensor.transpose(
                        BB[1][0:2 * G * EXP, tok(i)],
                        gates[:, i, :, :, :].rearrange("p s h e -> p (s h e)").bitcast(f32), ident[0:TP, 0:TP])
                last.then_inc(pe["gT"], 1)
                te.wait_ge(ac["gsT"], pair + 1)
                for e in range(EXP):
                    if e >= 3:
                        te.wait_ge(ac["gB"], EXP * pair + e - 2)
                    mm(GATE_BANK[e][:, 0:TW], spread[:, e, :], gsT[:, :],
                       start=True, stop=True).then_inc(pe["gB"], 1)

            def up(pair, n):
                e, h = n // G, n % G
                if n == 0:
                    te.wait_ge(po["x5T"], pair + 1)
                for c in range(HC):
                    if n:
                        te.wait_ge(ac["hid"], HC * (UNITS * pair + n - 1) + c + 1)
                    for part in range(2):
                        last = mm(HB[c][:, 0:TW], w1s[:, part, e, 128 * c:128 * (c + 1)], x5T[:, h, :],
                                  start=(part == 0), stop=(part == 1))
                    last.then_inc(pe["w1"], 1)

            def down(pair, e):
                te.wait_ge(ac["hid"], HC * G * (EXP * pair + e) + HC * G)
                if e == 0:
                    te.wait_ge(out_free, pair + 1)
                else:
                    te.wait_ge(ve_s["prod"], EXP * pair + e)
                for c in range(HC):
                    for h in range(G):
                        last = mm(YB[rows_of(h), 0:TT], w2[:, HC * e + c, :], hid[:, e % 2, h, c, :],
                                  start=(c == 0), stop=(c == HC - 1))
                last.then_inc(pe["y"], 1)

            def finish(pair):
                te.wait_ge(po["acc"], EXP * pair + EXP)
                back(YB, acc[:, EXP % 2, :], pe["out"])

            stages = {"A.win": win, "A.conv0": conv0, "A.conv1": conv1, "A.combine": combine, "A.t1": t1,
                      "A.proj": proj, "A.scores": scores, "A.v": values, "A.pv": pv, "A.t2": t2,
                      "A.router": router, "A.ffn_up": ffn_up, "A.ffn_down": ffn_down, "A.fback": fback, "B.t3": t3, "B.dx": dx,
                      "B.usum": usum, "B.eback": eback, "B.denoms": denoms, "B.carry": carry, "B.gram": gram, "B.linear": linear, "B.t4": t4,
                      "B.dy": dy, "B.embed": embed, "B.t5": t5, "B.logits": logits, "B.gates": gates_out}

            def experts(pair, name):
                if name == "XF":
                    finish(pair)
                elif name[0] == "X":
                    up(pair, int(name[1:]))
                elif name[0] == "Y":
                    down(pair, int(name[1:]))

            te.wait_ge(pack_in[0], 16)
            win(0)
            conv(0, 0)
            conv(1, 0)
            te.wait_ge(pack_in[1], 16)
            for h in range(G):
                last = mm(HB[0][rows_of(h), 0:D], wq, wk, start=True, stop=True)
            last.then_inc(wqk_mm, 1)
            combine(0)
            t1(0)
            te.wait_ge(wqk_set, 1)
            proj(0)
            scores(0)
            pv(0)
            values(0)
            t2(0)
            te.wait_ge(pack_in[2], 16)
            router(0)
            ffn_up(0)
            ffn_down(0)
            fback(0)
            te.wait_ge(spread_set, 1)

            def set_up(_, name):
                if name == "X0":
                    te.wait_ge(pack_in[3], 16)
                if name[0] == "X" and name != "XF":
                    n = int(name[1:])
                    e, c = n // HC, n % HC
                    mm(HB[1][:, n:n + 1], w1[0:D, e, 128 * c:128 * (c + 1)], bT[:, e:e + 1], start=True,
                       stop=True).then_inc(b1f_mm, 1)

            run(stages, set_up, a=1, b=0, x=0, order=RAMP)
            te.wait_ge(w1s_set, EXP)
            te.wait_ge(b1f_set, 1)
            with te.Fori(0, NP - 2) as pair:
                run(stages, experts, a=pair + 2, b=pair + 1, x=pair)
            run(stages, experts, b=NP - 1, x=NP - 2, order=DRAIN)
            run(stages, experts, x=NP - 1, order=DRAIN)

        @block.scalar
        def _(se):
            act = nc.scalar.activation

            def from_bank(dst, bank, pair, produced, done):
                se.wait_ge(produced, pair + 1)
                act(dst[:, :], bank[:, 0:TT], ACT.Copy).then_inc(done, 1)

            def win(pair):
                se.wait_ge(x_in, 32 * (pair + 1))
                for h in range(G):
                    for j in range(XJ):
                        last = act(xnat[:, h, j, :], xnat[:, h, j, :], ACT.Square,
                                   accum_out=sq[:, XJ * h + j:XJ * h + j + 1])
                last.then_inc(ac["sq"], 1)

            def conv(h, pair):
                se.wait_ge(pe["conv"], G * pair + h + 1)
                act(cs[0:D, h, :], AB[h][0:D, 0:TT], ACT.Copy).then_inc(ac["cslo"], 1)

            def conv0(pair):
                conv(0, pair)

            def conv1(pair):
                conv(1, pair)

            def t1(pair):
                from_bank(xnT, AB[0], pair, pe["t1"], ac["xnT"])

            def proj(pair):
                from_bank(gq, AB[1], pair, pe["proj"], ac["gq"])

            def softmax(pair):
                se.wait_ge(ve_s["nmax"], pair + 1)
                for h in range(G):
                    for i in range(NT):
                        q = tile_q(h, i)
                        last = act(probs[:, q, 0:SW[i]], probs[:, q, 0:SW[i]], ACT.Exp, bias=nmax[:, q:q + 1],
                                   accum_out=ssum[:, q:q + 1])
                    last.then_inc(ac["exp"], 1)

            def pv(pair):
                from_bank(attT, AB[0], pair, pe["pv"], ac["attT"])

            def t2(pair):
                from_bank(x2T, AB[0], pair, pe["t2"], ac["x2T"])

            def ffn_up(pair):
                for n in range(HC * G):
                    c, h = n // G, n % G
                    se.wait_ge(pe["f1"], HC * G * pair + n + 1)
                    act(hT[:, h, c, :], AB[h][:, 0:TT], ACT.Gelu_apprx_tanh,
                        bias=fb1[:, c:c + 1]).then_inc(ac["hT"], 1)

            def ffn_down(pair):
                se.wait_ge(pe["f2"], pair + 1)
                act(fyT[:, :], AB[0][:, 0:TT], ACT.Identity, bias=fb2[:, 0:1]).then_inc(ac["fyT"], 1)

            def t3(pair):
                from_bank(vT, BB[0], pair, pe["t3"], ac["vT"])

            def dx(pair):
                for n in range(HC * G):
                    h, c = n // HC, n % HC
                    se.wait_ge(pe["dx"], HC * G * pair + n + 1)
                    act(u[:, h, c, :], DX_BANK[n][:, 0:TT], ACT.Relu).then_inc(ac["u"], 1)

            def usum(pair):
                se.wait_ge(pe["usum"], pair + 1)
                act(us[:, :], BB[0][0:G, 0:TT], ACT.Copy, scale=1.0 / DECAY).then_inc(ac["us"], 1)

            def t4(pair):
                from_bank(naT, BB[0], pair, pe["t4"], ac["naT"])

            def embed(pair):
                from_bank(v_starT, BB[0], pair, pe["e"], ac["vstT"])

            def split(pair):
                se.wait_ge(ve_s["x5"], pair + 1)
                act(x5s[:, :, 0, :], x5[:, :, :], ACT.Copy).then_inc(ac["x5hi"], 1)

            def t5(pair):
                if not (isinstance(pair, int) and pair == 0):
                    se.wait_ge(po["x5T"], pair)
                for h in range(G):
                    se.wait_ge(pe["t5"], G * pair + h + 1)
                    act(x5N[:, h, 0:TT], BB[1 + h][:, 0:TT], ACT.Copy).then_inc(ac["x5N"], 1)

            def router_exp(pair):
                se.wait_ge(ve_s["lsub"], pair + 1)
                act(ex[:, :, :], lg[:, :, :], ACT.Exp).then_inc(ac["ex"], 1)

            def gates_out(pair):
                se.wait_ge(pe["gT"], pair + 1)
                act(gsT[:, 0:TT], BB[1][0:2 * G * EXP, 0:TT], ACT.Copy).then_inc(ac["gsT"], 1)
                if not (isinstance(pair, int) and pair == 0):
                    se.wait_ge(ve_s["prod"], EXP * pair)
                for e in range(EXP):
                    se.wait_ge(pe["gB"], EXP * pair + e + 1)
                    act(gateB[:, e, :], GATE_BANK[e][:, 0:TT], ACT.Copy).then_inc(ac["gB"], 1)

            def experts(pair, name):
                if name[0] != "X" or name == "XF":
                    return
                n = int(name[1:])
                e, h = n // G, n % G
                if e >= 2:
                    se.wait_ge(pe["y"], EXP * pair + e - 1)
                for c in range(HC):
                    se.wait_ge(pe["w1"], HC * (UNITS * pair + n) + c + 1)
                    act(hid[:, e % 2, h, c, :], HB[c][:, 0:TT], ACT.Gelu,
                        bias=b1f[:, HC * e + c:HC * e + c + 1]).then_inc(ac["hid"], 1)

            stages = {"A.win": win, "A.conv0": conv0, "A.conv1": conv1, "A.t1": t1, "A.proj": proj,
                      "A.exp": softmax, "A.pv": pv, "A.t2": t2, "A.ffn_up": ffn_up,
                      "A.ffn_down": ffn_down, "B.embed": embed, "B.t3": t3, "B.dx": dx,
                      "B.usum": usum, "B.t4": t4, "B.split": split, "B.t5": t5,
                      "B.ex": router_exp, "B.gates": gates_out}
            win(0)
            conv(0, 0)
            conv(1, 0)
            se.wait_ge(wqk_mm, 1)
            act(wqk[:, :], HB[0][:, 0:D], ACT.Copy).then_inc(wqk_set, 1)
            for stage in (t1, proj, softmax, pv, t2, ffn_up, ffn_down):
                stage(0)
            se.wait_ge(pack_in[2], 16)
            act(spread[:, :, :], field("spread").rearrange("p (e m) -> p e m", e=EXP),
                ACT.Copy).then_inc(spread_set, 1)
            run(stages, experts, a=1, b=0, order=RAMP)
            se.wait_ge(b1f_set, 1)
            with se.Fori(0, NP - 2) as pair:
                run(stages, experts, a=pair + 2, b=pair + 1, x=pair)
            run(stages, experts, b=NP - 1, x=NP - 2, order=DRAIN)
            run(stages, experts, x=NP - 1, order=DRAIN)

        @block.vector
        def _(dv):
            V = nc.vector

            def each(ap):
                return ap.unsqueeze(2).to_broadcast([TP, ap.shape[1], D])

            def ln_stats(n, source, pair):
                for q in range(Q):
                    last = V.bn_stats(stats[n][:, q, :], source(q))
                last.then_inc(ln_st[PHASE[n]], 1)
                dv.wait_ge(ln_st[PHASE[n]], ln_count(n, pair))
                dv.nop(nofuse=True)
                for q in range(Q):
                    last = V.bn_aggr(mv[n][:, q, :], stats[n][:, q, :])
                last.then_inc(ln_mv[n], 1)

            def center(n, source, pair):
                dv.wait_ge(ln_mv[n], pair + 1)
                V.tensor_tensor(xc[PHASE[n]][:, :, :], source, each(mv[n][:, :, 0]),
                                ALU.subtract).then_inc(ln_xc[PHASE[n]], 1)

            def normalise(n, pair):
                dv.wait_ge(ln_xc[PHASE[n]], ln_count(n, pair))
                dv.wait_ge(ln_rs[n], pair + 1)
                V.tensor_tensor(xn[n][:, :, :], xc[PHASE[n]][:, :, :], each(rstd[n][:, :]),
                                ALU.mult).then_inc(ln_xn[n], 1)

            def centered(n, source, pair):
                ln_stats(n, lambda q: source[:, q, :], pair)
                center(n, source, pair)

            def tiles(bank):
                return bank[0:TP, 0:Q * D].rearrange("p (q f) -> p q f", q=Q)

            def win(pair):
                dv.wait_ge(pe["win"], pair + 1)
                V.tensor_scalar(wn[:, :], AB[1][0:TP, 0:Q],
                                1e-7, None, ALU.add).then_inc(ve_s["wn"], 1)

            def conv(h, pair):
                dv.wait_ge(pe["conv"], G * pair + h + 1)
                V.tensor_copy(cs[D:128, h, :], AB[h][D:128, 1:TT + 1]).then_inc(ve_s["cshi"], 1)

            def conv0(pair):
                conv(0, pair)

            def conv1(pair):
                conv(1, pair)

            def combine(pair):
                dv.wait_ge(po["scale"], pair + 1)
                dv.wait_ge(pe["comb"], pair + 1)
                for q in range(Q):
                    last = V.scalar_tensor_tensor(res[0][:, q, :], AB[0][0:TP, D * q:D * (q + 1)],
                                                  cs_scale[:, q:q + 1], cbias[0:TP, :], ALU.mult, ALU.add)
                last.then_inc(ve_s["res0"], 1)
                dv.wait_ge(ve_s["res0"], pair + 1)
                centered(0, res[0][:, :, :], pair)

            def norm0(pair):
                normalise(0, pair)

            def scores(pair):
                for s in range(Q):
                    n = s % NT
                    q = tile_q(s // NT, n)
                    dv.wait_ge(pe["sc"], Q * pair + s + 1)
                    dv.nop(nofuse=True)
                    V.tensor_tensor_reduce(out=probs[:, q, 0:SW[n]], in0=AB[s % 2][0:TP, 0:SW[n]],
                                           in1=smask[:, sum(SW[:n]):sum(SW[:n + 1])], scale=D ** -0.5,
                                           scalar=-3.0e38, op0=ALU.add, op1=ALU.max,
                                           accum_out=smax[:, q:q + 1]).then_inc(ve_s["sc"], 1)
                dv.wait_ge(ve_s["sc"], Q * pair + Q)
                V.tensor_scalar(nmax[:, :], smax[:, :], -1.0, None, ALU.mult).then_inc(ve_s["nmax"], 1)

            def values(pair):
                dv.wait_ge(ac["exp"], G * pair + G)
                V.reciprocal(rsum[:, :], ssum[:, :]).then_inc(ve_s["rsum"], 1)
                dv.wait_ge(ve_s["rsum"], pair + 1)
                V.tensor_tensor(vv[:, :, :], xn[0][:, :, :], each(rsum[:, :]), ALU.mult).then_inc(ve_s["vv"], 1)

            def attended(pair):
                dv.wait_ge(pe["v"], pair + 1)
                for h in range(G):
                    last = V.tensor_tensor(res[1][:, h::G, :],
                                           AB[h][0:TP, 0:NT * D].rearrange("p (i f) -> p i f", i=NT),
                                           res[0][:, h::G, :], ALU.add)
                last.then_inc(ve_s["res1"], 1)
                dv.wait_ge(ve_s["res1"], pair + 1)
                centered(1, res[1][:, :, :], pair)

            def norm1(pair):
                normalise(1, pair)

            def diagonal(dst, row, h):
                for i in range(NT):
                    w = min(TP, T - TP * i)
                    last = V.tensor_tensor_reduce(out=ranks[:, tile_q(h, i), 0:w], in0=row[:, TP * i:TP * i + w],
                                                  in1=ident[0:TP, 0:w], scale=1.0, scalar=0.0, op0=ALU.mult,
                                                  op1=ALU.add, accum_out=dst[:, tile_q(h, i):tile_q(h, i) + 1])
                return last

            def router(pair):
                for h in range(G):
                    dv.wait_ge(pe["rt"], G * pair + h + 1)
                    V.tensor_scalar(wB[:, h, :], AB[h][0:TP, 0:T], brB[0:TP, 0:1], None,
                                    ALU.add).then_inc(ve_s["wB"], 1)

            def rank_tokens(pair):
                dv.wait_ge(ve_s["wB"], G * pair + G)
                for h in range(G):
                    last = diagonal(wcol, wB[:, h, :], h)
                last.then_inc(ve_s["wcol"], 1)
                dv.wait_ge(ve_s["wcol"], pair + 1)
                for h in range(G):
                    for i in range(NT):
                        q = tile_q(h, i)
                        last = V.scalar_tensor_tensor(ranks[:, q, 0:T], wB[:, h, :], wcol[:, q:q + 1], rankc[:, i, :],
                                                      ALU.subtract, ALU.is_ge, accum_out=rank[:, q:q + 1])
                last.then_inc(ve_s["rank"], 1)
                dv.wait_ge(ve_s["rank"], pair + 1)
                V.scalar_tensor_tensor(mw[:, :], rank[:, :], float(KEEP), wcol[:, :], ALU.is_lt,
                                       ALU.mult).then_inc(ve_s["mw"], 1)

            def ffn_down(pair):
                dv.wait_ge(pe["fb"], pair + 1)
                dv.wait_ge(ve_s["mw"], pair + 1)
                V.tensor_tensor(fy[:, :, :], tiles(AB[1]), each(mw[:, :]), ALU.mult).then_inc(ve_s["fy"], 1)
                dv.wait_ge(ve_s["fy"], pair + 1)
                dv.wait_ge(po["hx"], pair + 1)
                V.tensor_tensor(res[2][:, :, :], fy[:, :, :], hx[:, :, :], ALU.add).then_inc(ve_s["res2"], 1)
                dv.wait_ge(ve_s["res2"], pair + 1)
                centered(2, res[2][:, :, :], pair)

            def norm2(pair):
                normalise(2, pair)
                twice_var(2, "var3", pair)

            def twice_var(n, done, pair):
                V.tensor_tensor(twice[n][:, :], mv[n][:, :, 1], rstd[n][:, :], ALU.mult).then_inc(ve_s[done], 1)
                dv.wait_ge(ve_s[done], 2 * pair + 1)
                V.tensor_tensor(twice[n][:, :], twice[n][:, :], rstd[n][:, :], ALU.mult).then_inc(ve_s[done], 1)

            def usum(pair):
                dv.wait_ge(ac["us"], pair + 1)
                V.tensor_tensor_scan(seen[:, 4:TT + 4], us[:, :], us[:, :], 0.0, ALU.max,
                                     ALU.max).then_inc(ve_s["seen"], 1)
                V.tensor_scalar(ub[:, :], us[:, :], DECAY * 1e12, 1.0, ALU.mult, ALU.min).then_inc(ve_s["ub"], 1)
                dv.wait_ge(ve_s["seen"], pair + 1)
                V.tensor_scalar(grow[:, :], seen[:, 0:TT], 0.0, DECAY * 1e12, ALU.is_equal,
                                ALU.mult).then_inc(ve_s["grow"], 1)
                dv.wait_ge(ve_s["ub"], pair + 1)
                V.scalar_tensor_tensor(fed[:, :], seen[:, 1:TT + 1], 0.0, ub[:, :], ALU.is_gt,
                                       ALU.add).then_inc(ve_s["fed"], 1)
                dv.wait_ge(ve_s["fed"], pair + 1)
                V.tensor_tensor_scan(grown[:, 1:TT + 1], grow[:, :], fed[:, :], 0.0, ALU.mult,
                                     ALU.add).then_inc(ve_s["grown"], 1)
                dv.wait_ge(ve_s["grown"], pair + 1)
                V.scalar_tensor_tensor(den[:, :], grown[:, 0:TT], 1.0, us[:, :], ALU.min,
                                       ALU.add).then_inc(ve_s["den"], 1)
                dv.wait_ge(ve_s["den"], pair + 1)
                V.tensor_scalar(den2[:, :], den[:, :], 1e-12 / DECAY, None, ALU.max).then_inc(ve_s["guard"], 1)

            def denoms(pair):
                dv.wait_ge(pe["denT"], pair + 1)
                V.reciprocal(crow[:, :], BB[1][0:TP, 0:Q]).then_inc(ve_s["crow"], 1)
                dv.wait_ge(ve_s["crow"], pair + 1)
                V.tensor_tensor(cdiag[:, :, :], ident[0:TP, 0:TP].unsqueeze(1).to_broadcast([TP, Q, TP]),
                                crow[:, :].unsqueeze(2).to_broadcast([TP, Q, TP]), ALU.mult).then_inc(ve_s["cdiag"], 1)
                V.tensor_scalar(rt[:, :], crow[:, :], 1.0 / DECAY, None, ALU.mult).then_inc(ve_s["rt"], 1)
                dv.wait_ge(ve_s["rt"], pair + 1)
                V.tensor_tensor(rsq[:, :], rt[:, :], rt[:, :], ALU.mult).then_inc(ve_s["rsq"], 1)

            def carry(pair):
                for h in range(G):
                    dv.wait_ge(pe["carry"], G * pair + h + 1)
                    for c in range(HC):
                        last = V.tensor_tensor_scan(z[:, h, c, 1:TT], BB[2 * h][:, 0:TT - 1], u[:, h, c, 1:TT],
                                                    u[:, h, c, 0:1], ALU.mult, ALU.add)
                    last.then_inc(ve_s["z"], 1)

            def gram(pair):
                for n in range(2 * G):
                    h, k = n // 2, n % 2
                    dv.wait_ge(pe["gram"], 2 * G * pair + n + 1)
                    V.tensor_tensor(gd[:, h, TT * k:TT * (k + 1)], GRAM_BANK[n][0:TP, 0:TT],
                                    decay[:, TT * k:TT * (k + 1)], ALU.mult).then_inc(ve_s["gd"], 1)

            def linear(pair):
                dv.wait_ge(pe["a"], pair + 1)
                centered(4, tiles(BB[0]), pair)

            def norm4(pair):
                normalise(4, pair)

            def dy(pair):
                for n in range(HC * G):
                    h, c = n // HC, n % HC
                    dv.wait_ge(pe["dy"], HC * G * pair + n + 1)
                    V.scalar_tensor_tensor(yT[:, h, c, :], DX_BANK[n][:, 0:TT], 0.0, z[:, h, c, :],
                                           ALU.max, ALU.mult).then_inc(ve_s["yT"], 1)

            def embed(pair):
                dv.wait_ge(pe["eb"], pair + 1)
                centered(5, tiles(BB[1]), pair)

            def norm5(pair):
                normalise(5, pair)
                dv.wait_ge(ln_xn[5], pair + 1)
                if not (isinstance(pair, int) and pair == 0):
                    dv.wait_ge(po["keep"], pair)
                V.tensor_tensor(res[3][:, :, :], xn[5][:, :, :], res[2][:, :, :], ALU.add).then_inc(ve_s["res3"], 1)
                dv.wait_ge(ve_s["res3"], pair + 1)
                centered(6, res[3][:, :, :], pair)

            def twice6(pair):
                dv.wait_ge(ln_rs[6], pair + 1)
                twice_var(6, "var7", pair)

            def x5_out(pair):
                dv.wait_ge(ln_xc["B"], ln_count(6, pair))
                dv.wait_ge(po["lnsc"], pair + 1)
                V.tensor_tensor(x5[:, :, :], xc["B"][:, :, :], each(lnsc[:, :]), ALU.mult).then_inc(ve_s["x5"], 1)

            def split(pair):
                dv.wait_ge(ac["x5hi"], pair + 1)
                V.tensor_tensor(x5s[:, :, 1, :], x5[:, :, :], x5s[:, :, 0, :].bitcast(f32),
                                ALU.subtract).then_inc(ve_s["x5lo"], 1)

            def per_expert(ap):
                return ap.unsqueeze(2).to_broadcast([TP, Q, EXP])

            def logits(pair):
                dv.wait_ge(po["unagain"], pair + 1)
                dv.wait_ge(pe["lg"], pair + 1)
                V.tensor_tensor(lg[:, :, :], BB[0][0:TP, 0:Q * EXP].rearrange("p (q e) -> p q e", q=Q),
                                per_expert(unagain[:, :]), ALU.mult).then_inc(ve_s["lg"], 1)
                dv.wait_ge(ve_s["lg"], pair + 1)
                V.tensor_tensor(lg[:, :, :], lg[:, :, :], rb[0:TP, :].unsqueeze(1).to_broadcast([TP, Q, EXP]),
                                ALU.add).then_inc(ve_s["lb"], 1)
                dv.wait_ge(ve_s["lb"], pair + 1)
                V.reduce_max(lmax[:, :], lg[:, :, :], AX.X).then_inc(ve_s["lmax"], 1)
                dv.wait_ge(ve_s["lmax"], pair + 1)
                V.tensor_tensor(lg[:, :, :], lg[:, :, :], per_expert(lmax[:, :]),
                                ALU.subtract).then_inc(ve_s["lsub"], 1)

            def gate_out(pair):
                dv.wait_ge(ac["ex"], pair + 1)
                V.tensor_tensor(dif[:, :, :, :], ex[:, :, :].unsqueeze(2).to_broadcast([TP, Q, EXP, EXP]),
                                ex[:, :, :].unsqueeze(3).to_broadcast([TP, Q, EXP, EXP]),
                                ALU.subtract).then_inc(ve_s["dif"], 1)
                dv.wait_ge(ve_s["dif"], pair + 1)
                V.tensor_tensor(dif[:, :, :, :], dif[:, :, :, :],
                                topc[0:TP, :, :].unsqueeze(1).to_broadcast([TP, Q, EXP, EXP]),
                                ALU.is_ge).then_inc(ve_s["cmp"], 1)
                dv.wait_ge(ve_s["cmp"], pair + 1)
                V.reduce_sum(erank[:, :, :], dif[:, :, :, :], AX.X).then_inc(ve_s["erank"], 1)
                dv.wait_ge(ve_s["erank"], pair + 1)
                V.scalar_tensor_tensor(esel[:, :, :], erank[:, :, :], float(TOPK), ex[:, :, :], ALU.is_lt,
                                       ALU.mult).then_inc(ve_s["esel"], 1)
                dv.wait_ge(ve_s["esel"], pair + 1)
                V.reduce_sum(eden[:, :], esel[:, :, :], AX.X).then_inc(ve_s["eden"], 1)
                dv.wait_ge(ve_s["eden"], pair + 1)
                V.reciprocal(eden[:, :], eden[:, :]).then_inc(ve_s["erec"], 1)
                dv.wait_ge(ve_s["erec"], pair + 1)
                V.tensor_tensor(gate[:, :, :, :].rearrange("p i h e -> p (i h) e"), esel[:, :, :],
                                per_expert(eden[:, :]), ALU.mult).then_inc(ve_s["gate"], 1)
                dv.wait_ge(ve_s["gate"], pair + 1)
                V.tensor_copy(gates[:, :, 0, :, :], gate[:, :, :, :]).then_inc(ve_s["ghi"], 1)
                dv.wait_ge(ve_s["ghi"], pair + 1)
                V.tensor_tensor(gates[:, :, 1, :, :], gate[:, :, :, :], gates[:, :, 0, :, :].bitcast(f32),
                                ALU.subtract).then_inc(ve_s["glo"], 1)

            def experts(pair, name):
                if name[0] == "Z":
                    e = int(name[1:])
                    dv.wait_ge(pe["y"], EXP * pair + e + 1)
                    if e == 0:
                        dv.wait_ge(ac["gB"], EXP * pair + EXP)
                    if e >= 2:
                        dv.wait_ge(po["acc"], EXP * pair + e - 1)
                    V.scalar_tensor_tensor(prod[:, e % 2, :], YB[:, 0:TT], eb2[:, e:e + 1],
                                           gateB[:, e, :], ALU.add, ALU.mult).then_inc(ve_s["prod"], 1)
                if name == "XF":
                    dv.wait_ge(pe["out"], pair + 1)
                    dv.wait_ge(po["keep"], pair + 1)
                    dv.wait_ge(out_free, pair + 1)
                    V.tensor_tensor(outb[:, :, :], tiles(YB), keep[:, :, :], ALU.add).then_inc(ve_s["out"], 1)

            stages = {"A.win": win, "A.conv0": conv0, "A.conv1": conv1, "A.combine": combine, "A.norm0": norm0,
                      "A.scores": scores, "A.values": values, "A.v": attended, "A.norm1": norm1, "A.router": router,
                      "A.rank": rank_tokens, "A.fback": ffn_down, "A.norm2": norm2, "B.usum": usum,
                      "B.denoms": denoms, "B.carry": carry, "B.gram": gram, "B.linear": linear, "B.norm4": norm4,
                      "B.dy": dy, "B.eback": embed, "B.norm5": norm5, "B.twice6": twice6, "B.x5": x5_out,
                      "B.split": split, "B.logits": logits, "B.gate": gate_out}

            V.memset(mhalf[:, :], -0.5)
            V.memset(seen[:, 0:4], 0.0)
            V.memset(grown[:, 0:1], 0.0)
            V.memset(gsT[:, TT:TW].bitcast(f32), 0.0)
            V.memset(x5N[:, :, TT:TW].bitcast(f32), 0.0)
            V.memset(probs[:, :, T:TT], 0.0).then_inc(cst_set, 1)
            dv.wait_ge(pack_in[0], 16)
            for stage in (win, conv0, conv1, combine, norm0):
                stage(0)
            dv.wait_ge(pack_in[1], 16)
            dv.wait_ge(cst_set, 1)
            for stage in (scores, values, attended, norm1):
                stage(0)
            dv.wait_ge(pack_in[2], 16)
            for stage in (router, rank_tokens, ffn_down, norm2):
                stage(0)

            def set_up(_, name):
                if name == "XF":
                    dv.wait_ge(pack_in[3], 16)
                    dv.wait_ge(b1f_mm, EXP * HC)
                    V.tensor_tensor(b1f[:, :], HB[1][:, 0:EXP * HC], b1, ALU.add).then_inc(b1f_set, 1)

            run(stages, set_up, a=1, b=0, x=0, order=RAMP)
            with dv.Fori(0, NP - 2) as pair:
                run(stages, experts, a=pair + 2, b=pair + 1, x=pair)
            run(stages, experts, b=NP - 1, x=NP - 2, order=DRAIN)
            run(stages, experts, x=NP - 1, order=DRAIN)

        @block.gpsimd
        def _(gp):
            P = nc.gpsimd

            def root(n, pair):
                gp.wait_ge(ln_mv[n], pair + 1)
                gp.nop(nofuse=True)
                P.tensor_scalar(ve[n][:, :], mv[n][:, :, 1], LN_EPS, 1.0, ALU.add, ALU.mult).then_inc(ln_ve[n], 1)
                gp.wait_ge(ln_ve[n], pair + 1)
                P.tensor_tensor(rstd[n][:, :], ve[n][:, :], mhalf[0:TP, :], ALU.pow).then_inc(ln_rs[n], 1)

            def scaled_root(n, pair):
                gp.wait_ge(ln_mv[n], pair + 1)
                gp.wait_ge(ve_s["rsq"], pair + 1)
                P.tensor_tensor(ve[n][:, :], mv[n][:, :, 1], rsq[:, :], ALU.mult).then_inc(ln_ve[n], 1)
                gp.wait_ge(ln_ve[n], 3 * pair + 1)
                gp.nop(nofuse=True)
                P.tensor_scalar(vra[:, :], ve[n][:, :], LN_EPS, 1.0, ALU.add, ALU.mult).then_inc(ln_ve[n], 1)
                gp.wait_ge(ln_ve[n], 3 * pair + 2)
                P.tensor_tensor(vrb[:, :], vra[:, :], mhalf[0:TP, :], ALU.pow).then_inc(ln_ve[n], 1)
                gp.wait_ge(ln_ve[n], 3 * pair + 3)
                P.tensor_tensor(rstd[n][:, :], vrb[:, :], rt[:, :], ALU.mult).then_inc(ln_rs[n], 1)

            def win(pair):
                gp.wait_ge(ve_s["wn"], pair + 1)
                P.tensor_tensor(wr[:, :], wn[:, :], mhalf[0:TP, :], ALU.pow).then_inc(po["wr"], 1)
                gp.wait_ge(po["wr"], pair + 1)
                gp.nop(nofuse=True)
                P.tensor_scalar(cs_scale[:, :], wr[:, :], cscale[0:TP, 0:1], 1.0, ALU.mult,
                                ALU.mult).then_inc(po["scale"], 1)

            def combine(pair):
                root(0, pair)

            def pv(pair):
                root(1, pair)

            def norm1(pair):
                gp.wait_ge(ln_xn[1], pair + 1)
                P.tensor_tensor(hx[:, :, :], res[1][:, :, :], xn[1][:, :, :], ALU.add).then_inc(po["hx"], 1)

            def ffn_down(pair):
                root(2, pair)

            def norm2(pair):
                root_again(2, "var3", "again3", pair)

            def root_again(n, var, done, pair):
                gp.wait_ge(ve_s[var], 2 * pair + 2)
                gp.nop(nofuse=True)
                P.tensor_scalar(vrt[n][:, :], twice[n][:, :], LN_EPS, 1.0, ALU.add, ALU.mult).then_inc(po[done], 1)
                gp.wait_ge(po[done], 2 * pair + 1)
                P.tensor_tensor(again[n][:, :], vrt[n][:, :], mhalf[0:TP, :], ALU.pow).then_inc(po[done], 1)
                gp.wait_ge(po[done], 2 * pair + 2)

            def denoms(pair):
                gp.wait_ge(ac["u"], HC * G * pair + HC * G)
                gp.nop(nofuse=True)
                P.tensor_copy(z[:, :, :, 0:1], u[:, :, :, 0:1]).then_inc(po["z0"], 1)
                gp.wait_ge(ve_s["rt"], pair + 1)
                P.tensor_tensor(vrc[:, :], again[2][:, :], rt[:, :], ALU.mult).then_inc(po["lnvr"], 1)
                gp.wait_ge(ln_xn[2], pair + 1)
                gp.wait_ge(po["lnvr"], 2 * pair + 1)
                P.tensor_tensor(lnvr[:, :, :], xn[2][:, :, :], vrc[:, :].unsqueeze(2).to_broadcast([TP, Q, D]),
                                ALU.mult).then_inc(po["lnvr"], 1)

            def linear(pair):
                scaled_root(4, pair)

            def embed(pair):
                scaled_root(5, pair)

            def norm5(pair):
                root(6, pair)

            def twice6(pair):
                root_again(6, "var7", "again7", pair)
                P.tensor_tensor(lnsc[:, :], again[6][:, :], rstd[6][:, :], ALU.mult).then_inc(po["lnsc"], 1)
                P.tensor_tensor(unagain[:, :], again[6][:, :], vrt[6][:, :], ALU.mult).then_inc(po["unagain"], 1)

            def experts(pair, name):
                if name == "X0":
                    gp.wait_ge(ve_s["x5"], pair + 1)
                    gp.wait_ge(out_free, pair + 1)
                    gp.nop(nofuse=True)
                    P.tensor_copy(keep[:, :, :], res[3][:, :, :]).then_inc(po["keep"], 1)
                    gp.wait_ge(ac["x5N"], G * pair + G)
                    gp.nop(nofuse=True)
                    P.tensor_copy(x5T[:, :, :], x5N[:, :, :]).then_inc(po["x5T"], 1)
                if name[0] == "Z":
                    e = int(name[1:])
                    gp.wait_ge(ve_s["prod"], EXP * pair + e + 1)
                    if e == 0:
                        gp.nop(nofuse=True)
                        P.tensor_copy(acc[:, 1, :], prod[:, 0, :]).then_inc(po["acc"], 1)
                    else:
                        gp.wait_ge(po["acc"], EXP * pair + e)
                        P.tensor_tensor(acc[:, (e + 1) % 2, :], acc[:, e % 2, :], prod[:, e % 2, :],
                                        ALU.add).then_inc(po["acc"], 1)

            def set_up(_, name):
                if name == "X0":
                    gp.wait_ge(pack_in[3], 16)
                if name[0] == "Y":
                    e = int(name[1:])
                    P.tensor_tensor(w1g[:, e % 2, :], w1[:, e, :], gT[:, e:e + 1].to_broadcast([128, H]),
                                    ALU.mult).then_inc(w1g_set, 1)
                    gp.wait_ge(w1g_set, e + 1)
                    P.tensor_copy(w1s[:, 0, e, :], w1g[:, e % 2, :]).then_inc(w1hi_set, 1)
                    gp.wait_ge(w1hi_set, e + 1)
                    P.tensor_tensor(w1s[:, 1, e, :], w1g[:, e % 2, :], w1s[:, 0, e, :].bitcast(f32),
                                    ALU.subtract).then_inc(w1s_set, 1)
                    gp.wait_ge(w1s_set, e + 1)

            stages = {"A.win": win, "A.combine": combine, "A.v": pv, "A.norm1": norm1, "A.fback": ffn_down,
                      "A.norm2": norm2, "B.denoms": denoms, "B.linear": linear, "B.eback": embed,
                      "B.norm5": norm5, "B.twice6": twice6}
            gp.wait_ge(cst_set, 1)
            gp.wait_ge(pack_in[0], 16)
            run(stages, experts, a=0)
            run(stages, set_up, a=1, b=0, x=0, order=RAMP)
            with gp.Fori(0, NP - 2) as pair:
                run(stages, experts, a=pair + 2, b=pair + 1, x=pair)
            run(stages, experts, b=NP - 1, x=NP - 2, order=DRAIN)
            run(stages, experts, x=NP - 1, order=DRAIN)


def kernel(**inputs):
    import numpy as _np
    import concourse.bacc as _bacc
    from concourse import mybir as _mybir
    from concourse.bass_utils import run_bass_kernel_spmd as _run

    a = {k: _np.asarray(v) for k, v in inputs.items()}
    f = _np.float32
    x = a["x"]
    x_T = _np.zeros((CIN, B, XC), f)
    x_T[:, :, 0:L] = x.transpose(2, 0, 1)
    x_nat = _np.ascontiguousarray(x.reshape(B, XP, XJ, CIN).transpose(1, 0, 2, 3))

    def rows(v, n=128):
        return _np.broadcast_to(v.reshape(1, -1), (n, v.size))

    def halves(w):
        return w.reshape(HC, 128, -1).transpose(1, 0, 2).reshape(128, -1)

    def twice(w):
        return _np.concatenate([w, w])

    t = _np.arange(TT)
    band = _np.zeros((XP, XJ, TT), f)
    for j in range(XJ):
        d = XJ * _np.arange(XP)[:, None] + j - t[None, :]
        band[:, j] = (d >= 0) & (d < KW)
    smask = _np.concatenate([_np.where(t[None, :SW[i]] < (TP * i + _np.arange(TP))[:, None], 0.0, NEG)
                             for i in range(NT)], axis=1)
    rankc = _np.stack([_np.where(t[None, :T] < (TP * i + _np.arange(TP))[:, None], 0.0, TINY)
                       for i in range(NT)], axis=1)
    decay = []
    for i in range(NT):
        d = t[None, TP * i:] - (TP * i + _np.arange(TP))[:, None] - 1
        decay.append(_np.where(d >= 0, DECAY ** _np.maximum(d, 0).astype(_np.float64), 0.0))
    e = _np.arange(EXP)
    topc = _np.where(e[None, :] < e[:, None], 0.0, TINY)
    pick = _np.zeros((128, G, G), f)
    pick[:, range(G), range(G)] = 1.0
    pick = pick.reshape(128, -1)
    spread = _np.zeros((2, G, EXP, EXP, G, D), f)
    for h in range(G):
        spread[:, h, range(EXP), range(EXP), h, :] = 1.0
    spread = spread.reshape(2 * G * EXP, -1)

    values = {
        "conv": a["L0_tok_kernel"].transpose(1, 0, 2).reshape(CIN, KW * D),
        "eye2": _np.concatenate([_np.eye(D), _np.eye(D)]), "band": band.reshape(XP, -1),
        "cbias": rows(a["L0_tok_bias"]), "cscale": rows(a["L0_tok_scale"]),
        "ident": _np.eye(128), "wq": a["L0_attn_Wq"], "wk": a["L0_attn_Wk"], "wvT": twice(a["L0_attn_Wv"].T),
        "smask": smask, "wrB": twice(_np.broadcast_to(a["L0_ffn_wr"], (D, TP))), "brB": rows(a["L0_ffn_br"]),
        "rankc": rankc.reshape(TP, -1), "fw1": twice(a["L0_ffn_w1"]), "fb1": a["L0_ffn_b1"].reshape(HC, 128).T,
        "fw2": halves(a["L0_ffn_w2"]), "fb2": twice(a["L0_ffn_b2"].reshape(D, 1)),
        "dxT": twice(a["L1_attn_Dx"].T), "ones": _np.ones((128, 128)), "decay": _np.concatenate(decay, axis=1),
        "dyT": twice(a["L1_attn_Dy"].T), "eT": halves(a["L1_attn_E"].T), "rw": _np.concatenate([a["L1_ffn_Wr"]] * 2),
        "rb": rows(a["L1_ffn_br"]), "topc": rows(topc), "pick": pick, "spread": spread,
        "eb2": _np.concatenate([a["L1_ffn_b2"].T] * G),
        "w1": _np.concatenate([a["L1_ffn_W1"].transpose(1, 0, 2).reshape(D, -1)] * 2),
        "gT": _np.concatenate([a["L1_ffn_ln_g"].T] * 2),
        "bT": a["L1_ffn_ln_b"].T, "b1": a["L1_ffn_b1"].reshape(EXP * HC, 128).T,
        "w2": a["L1_ffn_W2"].reshape(EXP * HC, 128, D).transpose(1, 0, 2).reshape(128, -1),
    }
    at, widths = fields()
    packs = [_np.zeros((128, w), f) for w in widths]
    for name, v in values.items():
        n, c, cols, nrows = at[name]
        packs[n][0:nrows, c:c + v.shape[1]] = v

    nc = _bacc.Bacc("TRN2", target_bir_lowering=False, num_devices=1)
    arrays = {"in_x_nat": x_nat, "in_x_T": x_T} | {f"in_pack{n}": p for n, p in enumerate(packs)}
    aps = {n: nc.dram_tensor(n, v.shape, _mybir.dt.from_np(v.dtype), kind="ExternalInput").ap()
           for n, v in arrays.items()}
    out = nc.dram_tensor("out_0_dram", (TP, B * NT, D), _mybir.dt.float32, kind="ExternalOutput").ap()
    build(nc, aps["in_x_nat"], aps["in_x_T"], [aps[f"in_pack{n}"] for n in range(len(packs))], out)
    r = _run(nc, [arrays], core_ids=[0])
    got = r.results[0]["out_0_dram"]
    return _np.ascontiguousarray(
        got.reshape(TP, NP, NT, G, D).transpose(1, 3, 2, 0, 4).reshape(B, TT, D)[:, :T])
```
